# Optimizing a Trainium2 kernel written in Bass

```python
import numpy as np
import jax
import jax.numpy as jnp

def _softmax(x, axis=-1):
    return jax.nn.softmax(x, axis=axis)

def _gelu(x):
    return jax.nn.gelu(x, approximate=True)

def _silu(x):
    return jax.nn.silu(x)

def _sigmoid(x):
    return jax.nn.sigmoid(x)

def _layernorm(x, axis=-1, eps=1e-05):
    m = jnp.mean(x, axis=axis, keepdims=True)
    v = jnp.var(x, axis=axis, keepdims=True)
    return (x - m) / jnp.sqrt(v + eps)

def _scatter_add(tgt, idx, src, axis=0):
    return tgt.at[idx].add(src)

def _segment_sum(src, seg, n):
    return jax.ops.segment_sum(src, seg, n)
kernel_name = 'mk_early_fusion_d2_tok_img256_r4_7f3a3f'

def setup_inputs(seed: int=0):
    np.random.seed(seed)
    _w = jnp.asarray

    def _rec_inputs():
        import jax
        import jax.numpy as jnp
        _rk = jax.random.key(seed)
        x = -7.10856e-05 + 0.999911 * jax.random.normal(jax.random.fold_in(_rk, 1), (128, 1, 84, 84), jnp.float32)
        txt = 7.83249e-05 + 0.02 * jax.random.normal(jax.random.fold_in(_rk, 2), (128, 32, 64), jnp.float32)
        return (x, txt)
    x, txt = _rec_inputs()

    def _L0_tok_setup():
        import jax, jax.numpy as jnp
        import numpy as np
        INV_SQRT2 = 0.7071067811865476

        def haar_dwt2(x):
            lo = (x[..., ::2] + x[..., 1::2]) * INV_SQRT2
            hi = (x[..., ::2] - x[..., 1::2]) * INV_SQRT2
            cA = (lo[..., ::2, :] + lo[..., 1::2, :]) * INV_SQRT2
            cH = (lo[..., ::2, :] - lo[..., 1::2, :]) * INV_SQRT2
            cV = (hi[..., ::2, :] + hi[..., 1::2, :]) * INV_SQRT2
            cD = (hi[..., ::2, :] - hi[..., 1::2, :]) * INV_SQRT2
            return (cA, (cH, cV, cD))

        def wavedec2_maps(x, levels):
            a = x
            details = []
            for _ in range(levels):
                a, d = haar_dwt2(a)
                details.append(d)
            maps = [a]
            for d in reversed(details):
                maps.extend(d)
            return maps
        key = jax.random.key(seed)
        k1, k2 = jax.random.split(key)
        B, H, W_img = (64, 256, 256)
        x = jax.random.normal(k1, (B, 1, H, W_img), dtype=jnp.float32)
        n_maps = 1 + 3 * 2
        W = jax.random.normal(k2, (n_maps, 64), dtype=jnp.float32) * (1.0 / np.sqrt(n_maps))
        b = jnp.zeros((64,), dtype=jnp.float32)
        return {'x': x, 'W': W, 'b': b}
    _L0_tok_all = _L0_tok_setup()
    _L0_tok_in = {k: v for k, v in _L0_tok_all.items() if k in ('W', 'b')}
    del _L0_tok_all

    def _L0_attn_setup():
        import jax, jax.numpy as jnp
        import numpy as np
        B, L, H, C, D = (16, 1024, 64, 1, 64)

        def krylov(L, A, b, c):
            x = b[..., None]
            A_ = A
            while x.shape[-1] < L:
                x = jnp.concatenate([x, jnp.einsum('chij,chjt->chit', A_, x)], axis=-1)
                A_ = jnp.einsum('chij,chjk->chik', A_, A_)
            x = x[..., :L]
            return jnp.einsum('chd,chdl->chl', c, x)
        key = jax.random.key(seed)
        k1, k2 = jax.random.split(key)
        u = jax.random.normal(k1, (B, L, H), dtype=jnp.float32)
        c = jax.random.normal(k2, (C, H, D), dtype=jnp.float32)
        return {'u': u, 'c': c}
    _L0_attn_all = _L0_attn_setup()
    _L0_attn_in = {k: v for k, v in _L0_attn_all.items() if k in ('c',)}
    del _L0_attn_all

    def _L0_ffn_setup():
        import jax, jax.numpy as jnp
        import numpy as np
        NUM_EXPERTS = 8
        TOP_K = 2
        B, S, D = (8, 2048, 64)

        def _moe(tokens, router_w, w1, b1, w2, b2):
            N = tokens.shape[0]
            E = router_w.shape[0]
            logits = tokens.astype(jnp.float32) @ router_w.astype(jnp.float32).T
            probs = jax.nn.softmax(logits, axis=-1)
            rw, re = jax.lax.top_k(probs, TOP_K)
            if TOP_K > 1:
                rw = rw / jnp.maximum(rw.sum(-1, keepdims=True), 1e-12)
            rw = rw.astype(tokens.dtype)
            combine = jnp.zeros((N, E), tokens.dtype).at[jnp.arange(N)[:, None], re].set(rw)
            out = tokens
            for e in range(E):
                h = jax.nn.gelu(tokens @ w1[e] + b1[e], approximate=False)
                y = h @ w2[e] + b2[e]
                out = out + combine[:, e:e + 1] * y
            return out
        key = jax.random.key(seed)
        ks = jax.random.split(key, 4)
        scale = 1.0 / np.sqrt(D).astype(np.float32)
        return {'input_embeddings': jax.random.normal(ks[0], (B, S, D), jnp.float32), 'router_w': jax.random.normal(ks[1], (NUM_EXPERTS, D), jnp.float32) * scale, 'w1': jax.random.normal(ks[2], (NUM_EXPERTS, D, D), jnp.float32) * scale, 'b1': jnp.zeros((NUM_EXPERTS, D), jnp.float32), 'w2': jax.random.normal(ks[3], (NUM_EXPERTS, D, D), jnp.float32) * scale, 'b2': jnp.zeros((NUM_EXPERTS, D), jnp.float32)}
    _L0_ffn_all = _L0_ffn_setup()
    _L0_ffn_in = {k: v for k, v in _L0_ffn_all.items() if k in ('router_w', 'w1', 'b1', 'w2', 'b2')}
    del _L0_ffn_all

    def _L1_attn_setup():
        import jax, jax.numpy as jnp
        import numpy as np
        B, S, F, H = (4, 256, 64, 8)
        SCALE = float(F) ** 0.5
        key = jax.random.key(seed)
        ks = jax.random.split(key, 5)
        return {'q_input': jax.random.normal(ks[0], (B, S, F), dtype=jnp.float32), 'Wq': jax.random.normal(ks[1], (F, F * H), dtype=jnp.float32) * 0.02, 'Wk': jax.random.normal(ks[2], (F, F * H), dtype=jnp.float32) * 0.02, 'Wv': jax.random.normal(ks[3], (F, F * H), dtype=jnp.float32) * 0.02, 'Wo': jax.random.normal(ks[4], (F * H, F), dtype=jnp.float32) * 0.02}
    _L1_attn_all = _L1_attn_setup()
    _L1_attn_in = {k: v for k, v in _L1_attn_all.items() if k in ('Wq', 'Wk', 'Wv', 'Wo')}
    del _L1_attn_all

    def _L1_ffn_setup():
        import jax, jax.numpy as jnp
        import numpy as np
        C = 64
        HID = 256
        E = 8
        TEMP = 1.0
        key = jax.random.key(seed)
        ks = jax.random.split(key, 7)
        x = jax.random.normal(ks[0], (8, 4096, C), dtype=jnp.float32)
        W1 = jax.random.normal(ks[1], (C, HID), dtype=jnp.float32) * 0.02
        b1 = jnp.zeros((HID,), dtype=jnp.float32)
        Wg = jax.random.normal(ks[2], (HID, E), dtype=jnp.float32) * 0.02
        bg = jnp.zeros((E,), dtype=jnp.float32)
        Wd = jax.random.normal(ks[3], (E, HID, C), dtype=jnp.float32) * 0.02
        bd = jnp.zeros((E, C), dtype=jnp.float32)
        return {'x': x, 'W1': W1, 'b1': b1, 'Wg': Wg, 'bg': bg, 'Wd': Wd, 'bd': bd}
    _L1_ffn_all = _L1_ffn_setup()
    _L1_ffn_in = {k: v for k, v in _L1_ffn_all.items() if k in ('W1', 'b1', 'Wg', 'bg', 'Wd', 'bd')}
    del _L1_ffn_all
    return {'x': x, 'txt': txt, 'L0_tok_W': _L0_tok_in['W'], 'L0_tok_b': _L0_tok_in['b'], 'L0_attn_c': _L0_attn_in['c'], 'L0_ffn_router_w': _L0_ffn_in['router_w'], 'L0_ffn_w1': _L0_ffn_in['w1'], 'L0_ffn_b1': _L0_ffn_in['b1'], 'L0_ffn_w2': _L0_ffn_in['w2'], 'L0_ffn_b2': _L0_ffn_in['b2'], 'L1_attn_Wq': _L1_attn_in['Wq'], 'L1_attn_Wk': _L1_attn_in['Wk'], 'L1_attn_Wv': _L1_attn_in['Wv'], 'L1_attn_Wo': _L1_attn_in['Wo'], 'L1_ffn_W1': _L1_ffn_in['W1'], 'L1_ffn_b1': _L1_ffn_in['b1'], 'L1_ffn_Wg': _L1_ffn_in['Wg'], 'L1_ffn_bg': _L1_ffn_in['bg'], 'L1_ffn_Wd': _L1_ffn_in['Wd'], 'L1_ffn_bd': _L1_ffn_in['bd']}

def reference(x, txt, L0_tok_W, L0_tok_b, L0_attn_c, L0_ffn_router_w, L0_ffn_w1, L0_ffn_b1, L0_ffn_w2, L0_ffn_b2, L1_attn_Wq, L1_attn_Wk, L1_attn_Wv, L1_attn_Wo, L1_ffn_W1, L1_ffn_b1, L1_ffn_Wg, L1_ffn_bg, L1_ffn_Wd, L1_ffn_bd):
    import jax
    import jax.numpy as jnp

    def _L0_tok_ref(x, W, b):
        import jax, jax.numpy as jnp
        import numpy as np
        INV_SQRT2 = 0.7071067811865476

        def haar_dwt2(x):
            lo = (x[..., ::2] + x[..., 1::2]) * INV_SQRT2
            hi = (x[..., ::2] - x[..., 1::2]) * INV_SQRT2
            cA = (lo[..., ::2, :] + lo[..., 1::2, :]) * INV_SQRT2
            cH = (lo[..., ::2, :] - lo[..., 1::2, :]) * INV_SQRT2
            cV = (hi[..., ::2, :] + hi[..., 1::2, :]) * INV_SQRT2
            cD = (hi[..., ::2, :] - hi[..., 1::2, :]) * INV_SQRT2
            return (cA, (cH, cV, cD))

        def wavedec2_maps(x, levels):
            a = x
            details = []
            for _ in range(levels):
                a, d = haar_dwt2(a)
                details.append(d)
            maps = [a]
            for d in reversed(details):
                maps.extend(d)
            return maps
        imgs = x[:, 0]
        B = imgs.shape[0]
        maps = wavedec2_maps(imgs, 2)
        proc = [jax.image.resize(m, (B, 8, 8), method='bilinear') for m in maps]
        feat = jnp.stack(proc, axis=1)
        feat = feat.reshape(B, feat.shape[1], 64).transpose(0, 2, 1)
        return feat @ W + b

    def _L0_attn_ref(u, c):
        import jax, jax.numpy as jnp
        import numpy as np
        B, L, H, C, D = (16, 1024, 64, 1, 64)

        def krylov(L, A, b, c):
            x = b[..., None]
            A_ = A
            while x.shape[-1] < L:
                x = jnp.concatenate([x, jnp.einsum('chij,chjt->chit', A_, x)], axis=-1)
                A_ = jnp.einsum('chij,chjk->chik', A_, A_)
            x = x[..., :L]
            return jnp.einsum('chd,chdl->chl', c, x)
        Cc, Hh, Dd = c.shape
        A = jnp.zeros((Dd, Dd), c.dtype).at[1:, :-1].set(jnp.eye(Dd - 1, dtype=c.dtype))
        A = jnp.broadcast_to(A, (Cc, Hh, Dd, Dd))
        b = jnp.zeros((Dd,), c.dtype).at[0].set(1.0)
        b = jnp.broadcast_to(b, (Cc, Hh, Dd))
        ub = jnp.transpose(u, (0, 2, 1))
        l = ub.shape[-1]
        f = krylov(l, A, b, c)
        n = 2 * l
        u_f = jnp.fft.rfft(ub, n=n)
        v_f = jnp.fft.rfft(f, n=n)
        y_f = jnp.einsum('bhl,chl->bchl', u_f, v_f)
        y = jnp.fft.irfft(y_f, n=n)[..., :l]
        y = y.reshape(y.shape[0], -1, l)
        return jnp.transpose(y, (0, 2, 1))

    def _L0_ffn_ref(input_embeddings, router_w, w1, b1, w2, b2):
        import jax, jax.numpy as jnp
        import numpy as np
        NUM_EXPERTS = 8
        TOP_K = 2
        B, S, D = (8, 2048, 64)

        def _moe(tokens, router_w, w1, b1, w2, b2):
            N = tokens.shape[0]
            E = router_w.shape[0]
            logits = tokens.astype(jnp.float32) @ router_w.astype(jnp.float32).T
            probs = jax.nn.softmax(logits, axis=-1)
            rw, re = jax.lax.top_k(probs, TOP_K)
            if TOP_K > 1:
                rw = rw / jnp.maximum(rw.sum(-1, keepdims=True), 1e-12)
            rw = rw.astype(tokens.dtype)
            combine = jnp.zeros((N, E), tokens.dtype).at[jnp.arange(N)[:, None], re].set(rw)
            out = tokens
            for e in range(E):
                h = jax.nn.gelu(tokens @ w1[e] + b1[e], approximate=False)
                y = h @ w2[e] + b2[e]
                out = out + combine[:, e:e + 1] * y
            return out
        b, s, d = input_embeddings.shape
        tokens = input_embeddings.reshape(b * s, d)
        return _moe(tokens, router_w, w1, b1, w2, b2).reshape(b, s, d)

    def _L1_attn_ref(q_input, Wq, Wk, Wv, Wo):
        import jax, jax.numpy as jnp
        import numpy as np
        B, S, F, H = (4, 256, 64, 8)
        SCALE = float(F) ** 0.5
        b, s, f = q_input.shape
        h = Wq.shape[1] // f
        q = (q_input.reshape(b * s, f) @ Wq).reshape(b, s, f, h)
        k = (q_input.reshape(b * s, f) @ Wk).reshape(b, s, f, h)
        v = (q_input.reshape(b * s, f) @ Wv).reshape(b, s, f, h)
        qkt = jnp.einsum('bifh,bjfh->bijh', q, k)
        attn = jax.nn.sigmoid(qkt * SCALE)
        wv = jnp.einsum('bijh,bjfh->bifh', attn, v)
        wv = wv.reshape(b * s, f * h)
        out = jax.nn.relu(wv @ Wo)
        return out.reshape(b, s, f)

    def _L1_ffn_ref(x, W1, b1, Wg, bg, Wd, bd):
        import jax, jax.numpy as jnp
        import numpy as np
        C = 64
        HID = 256
        E = 8
        TEMP = 1.0
        orig_shape = x.shape
        xf = x.reshape(-1, orig_shape[-1])
        H = jax.nn.gelu(xf @ W1 + b1, approximate=False)
        probs = jax.nn.softmax((H @ Wg + bg) / TEMP, axis=-1)
        assign = jnp.argmax(probs, axis=-1)
        out = jnp.zeros_like(xf)
        for e in range(Wd.shape[0]):
            y = H @ Wd[e] + bd[e]
            sel = (assign == e)[:, None]
            out = out + jnp.where(sel, probs[:, e:e + 1] * y, 0.0)
        return out.reshape(orig_shape)
    h = _L0_tok_ref(x, L0_tok_W, L0_tok_b)
    h = jnp.concatenate([h, txt], axis=1)
    h = h + _L0_attn_ref(_layernorm(h, axis=-1), L0_attn_c)
    h = h + _L0_ffn_ref(_layernorm(h, axis=-1), L0_ffn_router_w, L0_ffn_w1, L0_ffn_b1, L0_ffn_w2, L0_ffn_b2)
    h = h + _L1_attn_ref(_layernorm(h, axis=-1), L1_attn_Wq, L1_attn_Wk, L1_attn_Wv, L1_attn_Wo)
    h = h + _L1_ffn_ref(_layernorm(h, axis=-1), L1_ffn_W1, L1_ffn_b1, L1_ffn_Wg, L1_ffn_bg, L1_ffn_Wd, L1_ffn_bd)
    return h

_drawn_inputs = setup_inputs


def setup_inputs(seed=0):
    import zlib

    import numpy as np

    out = dict(_drawn_inputs(seed))
    spreads = {'L0_tok_b': (0.0, 0.1),
     'L0_ffn_b1': (0.0, 0.8),
     'L0_ffn_b2': (0.0, 0.8),
     'L1_ffn_b1': (0.0, 0.8),
     'L1_ffn_bg': (0.0, 0.8),
     'L1_ffn_bd': (0.0, 0.8)}
    factors = {'L1_ffn_W1': 8.0, 'L1_ffn_Wg': 8.0, 'L1_ffn_Wd': 8.0}
    for name, (base, spread) in spreads.items():
        noise = np.random.default_rng([zlib.crc32(name.encode()), seed]).standard_normal(out[name].shape)
        drawn = base * np.exp(spread * noise) if base else spread * noise
        out[name] = jnp.asarray(drawn.astype(out[name].dtype))
    for name, factor in factors.items():
        out[name] = (out[name] * factor).astype(out[name].dtype)
    return out
```

```python
import numpy as np
from contextlib import ExitStack

import concourse.bass as bass
from concourse import mybir

F32 = mybir.dt.float32
F32R = mybir.dt.float32r
ALU = mybir.AluOpType
ACT = mybir.ActivationFunctionType
AX_X = mybir.AxisListType.X

B = 128
IMG = 84
G8 = 8
T = 96
TI = G8 * G8
D = 64
NMAP = 7
NE = 8
HEADS = 8
GB = 4
GT = GB * T
NG = B // GB
CH = NE * D // 128
HID = 256
HC = HID // 128
LB = 16
NLG = B // LB
EPS = 1e-5


def halves(ap, n):
    return ap.rearrange("p (b x) -> p b x", b=n)


def backwards(ap):
    *outer, (step, n) = [list(d) for d in ap.ap]
    return bass.AP(tensor=ap.tensor, offset=ap.offset + (n - 1) * step, ap=[*outer, [-step, n]])


def over(ap, n):
    return ap.unsqueeze(2).to_broadcast([ap.shape[0], ap.shape[1], n])



class Norm:

    def __init__(self, sb, sem, tag, nb):
        def two(name, cols):
            return [sb(f"{tag}_{name}{i}", [T, cols], F32) for i in range(2)]

        self.nb = nb
        self.total, self.power, self.variance, self.rstd = (two(n, nb) for n in ("total", "power", "variance", "rstd"))
        self.centred, self.square = two("centred", nb * D), two("square", nb * D)
        self.summed = sem(f"{tag}_summed")
        self.centred_ready = sem(f"{tag}_centred")
        self.squared = sem(f"{tag}_squared")
        self.power_ready = sem(f"{tag}_power")
        self.variance_ready = sem(f"{tag}_variance")
        self.rstd_ready = sem(f"{tag}_rstd")
        self.normed = sem(f"{tag}_normed")


def norm_sum(nc, dve, L, h, q):
    nc.vector.tensor_reduce(L.total[q][:, :], h, axis=AX_X, op=ALU.add).then_inc(L.summed, 1)


def norm_centre(nc, dve, L, h, t, q):
    dve.wait_ge(L.summed, t + 1)
    nc.vector.scalar_tensor_tensor(out=halves(L.centred[q][:, :], L.nb), in0=over(L.total[q][:, :], D),
                                   scalar=-1.0 / D, in1=h, op0=ALU.mult, op1=ALU.add).then_inc(L.centred_ready, 1)


def norm_square(nc, act, L, t, q):
    act.wait_ge(L.centred_ready, t + 1)
    nc.scalar.activation(L.square[q][:, :], L.centred[q][:, :], ACT.Square).then_inc(L.squared, 1)


def norm_power(nc, dve, L, t, q):
    dve.wait_ge(L.squared, t + 1)
    nc.vector.tensor_reduce(L.power[q][:, :], halves(L.square[q][:, :], L.nb), axis=AX_X,
                            op=ALU.add).then_inc(L.power_ready, 1)


def norm_rstd(nc, pool, L, consts, t, q):
    pool.wait_ge(L.power_ready, t + 1)
    nc.gpsimd.tensor_tensor(L.variance[q][:, :], L.power[q][:, :], consts[1][:, 0:L.nb],
                            ALU.add).then_inc(L.variance_ready, 1)
    pool.wait_ge(L.variance_ready, t + 1)
    nc.gpsimd.tensor_tensor(L.rstd[q][:, :], L.variance[q][:, :], consts[0][:, 0:L.nb],
                            ALU.pow).then_inc(L.rstd_ready, 1)


def norm_scale(nc, dve, L, out, t, q):
    dve.wait_ge(L.rstd_ready, t + 1)
    nc.vector.scalar_tensor_tensor(out=out, in0=halves(L.centred[q][:, :], L.nb), scalar=float(D) ** 0.5,
                                   in1=over(L.rstd[q][:, :], D), op0=ALU.mult, op1=ALU.mult).then_inc(L.normed, 1)



class Split:

    def __init__(self, sb, sem, tag, nb):
        self.nb = nb
        self.pair = [sb(f"{tag}_pair{i}", [T, nb * 2 * D], F32R) for i in range(2)]
        self.high = sem(f"{tag}_high")
        self.low = sem(f"{tag}_low")
        self.turned = sem(f"{tag}_turned")
        self.stored = sem(f"{tag}_stored")


def part(S, q, i):
    return S.pair[q][:, :].rearrange("p (b two x) -> p b two x", b=S.nb, two=2)[:, :, i, :]


def split_high(nc, act, L, S, xn, t, q):
    act.wait_ge(L.normed, t + 1)
    nc.scalar.activation(part(S, q, 0), xn, ACT.Copy).then_inc(S.high, 1)


def split_low(nc, dve, S, xn, t, q):
    dve.wait_ge(S.high, t + 1)
    nc.vector.tensor_tensor(part(S, q, 1), xn, part(S, q, 0).bitcast(F32), ALU.subtract).then_inc(S.low, 1)


def split_turn(nc, pe, S, ident, ps, t, q, first, n):
    for b in range(n):
        last = nc.tensor.transpose(ps[:, b * T:(b + 1) * T],
                                   S.pair[q][:, (first + b) * 2 * D:(first + b + 1) * 2 * D].bitcast(F32),
                                   ident[0:T, 0:T])
    last.then_inc(S.turned, 1)



def prepare(nc, sb, pb, sem, A, P):
    with ExitStack() as tmp:
        def scratch(name, shape, dt=F32):
            return tmp.enter_context(nc.sbuf_tensor(name, shape, dt))

        up = scratch("up_raw", [128, NE * D])
        router = scratch("router_raw", [128, NE])
        wq, wk, wv = (scratch(f"{n}_raw", [128, D * HEADS]) for n in ("wq", "wk", "wv"))
        wo = scratch("wo_raw", [D, HEADS * D])
        turned = [scratch(f"{n}_turned", [D, HEADS * 128]) for n in ("wq", "wk", "wv")]
        fold = scratch("fold", [128, HEADS * D])
        up2 = scratch("up2_raw", [128, HID])
        gate2 = scratch("gate2_raw", [128, HC * NE])
        down2 = scratch("down2_raw", [128, HC * NE * D])
        bias_row = scratch("bd_raw", [1, NE * D])
        bias_low = scratch("bd_low", [1, NE * D])
        ones = scratch("ones_raw", [128, 128])
        zeros = scratch("zeros_raw", [128, 512])
        taps = scratch("taps", [D, D])
        cpad = scratch("cpad", [D, 2 * T])
        sel_raw = scratch("sel_raw", [2 * NE, CH * 128])
        ps = [pb(f"prep_ps{i}", [128, 512]) for i in range(8)]

        loaded = sem("weights_loaded")
        padded = sem("filter_padded")
        reversed_taps = sem("filter_reversed")
        zeroed = sem("weights_zeroed")
        wt = sem("weights_turned")
        wc = sem("weights_copied")
        folded = sem("weights_folded")
        split = sem("weights_split")

        w1 = A["L0_ffn_w1"].rearrange("e d f -> d e f")
        loads = []
        for s in range(2):
            at = slice(s * D, (s + 1) * D)
            loads += [(up[at, :].rearrange("p (e f) -> p e f", e=NE), w1),
                      (router[at, :], A["L0_ffn_router_w"].rearrange("e d -> d e")),
                      (wq[at, :], A["L1_attn_Wq"]), (wk[at, :], A["L1_attn_Wk"]), (wv[at, :], A["L1_attn_Wv"]),
                      (up2[at, :], A["L1_ffn_W1"])]
        loads += [(wo[:, :], A["L1_attn_Wo"].rearrange("(u h) c -> u (h c)", h=HEADS)),
                  (P["down"][:, :].rearrange("p (k c) -> p k c", k=CH),
                   A["L0_ffn_w2"].rearrange("(k two) f c -> (two f) k c", two=2)),
                  (P["up_bias"][:, :], A["L0_ffn_b1"].rearrange("(k two) f -> (two f) k", two=2)),
                  (P["down_bias"][0:NE, :], A["L0_ffn_b2"]), (P["down_bias"][NE:2 * NE, :], A["L0_ffn_b2"]),
                  (P["up2_bias"][:, :], A["L1_ffn_b1"].rearrange("(k p) -> p k", p=128)),
                  (gate2[:, :].rearrange("p (k e) -> p k e", k=HC), A["L1_ffn_Wg"].rearrange("(k p) e -> p k e", p=128)),
                  (P["gate2_bias"][:, :], A["L1_ffn_bg"].unsqueeze(0).to_broadcast([T, NE])),
                  (bias_row[:, :].rearrange("a (e c) -> a e c", e=NE), A["L1_ffn_bd"].unsqueeze(0)),
                  (P["ident"][:, :], A["c_ident"]), (P["rank"][:, :], A["c_rank"]),
                  (sel_raw[:, :], A["c_sel"]), (taps[:, :], A["L0_attn_c"][0])]
        for k in range(HC):
            loads.append((down2[:, k * NE * D:(k + 1) * NE * D].rearrange("p (e c) -> p e c", e=NE),
                          A["L1_ffn_Wd"][:, k * 128:(k + 1) * 128, :].rearrange("e p c -> p e c")))
        n_loads = len(loads) * 16

        with nc.Block() as block:
            @block.sync
            def _(sp):
                with nc.allow_non_contiguous_dma(reason="a few small transposed weights"):
                    for dst, src in loads:
                        sp.dma_start(dst, src).then_inc(loaded, 16)
                sp.wait_ge(reversed_taps, 1)
                sp.dma_start(P["cpad_dram"], cpad[:, :]).then_inc(padded, 16)
                sp.wait_ge(padded, 16)
                sp.wait_ge(loaded, n_loads)

            @block.gpsimd
            def _(pool):
                nc.gpsimd.memset(ones[:, :], 1.0).then_inc(zeroed, 1)
                nc.gpsimd.memset(zeros[:, :], 0.0).then_inc(zeroed, 1)
                nc.gpsimd.memset(cpad[:, :], 0.0).then_inc(zeroed, 1)
                nc.gpsimd.memset(P["norm_consts"][0][:, :], -0.5)
                nc.gpsimd.memset(P["norm_consts"][1][:, :], D * EPS)

            @block.tensor
            def _(pe):
                pe.wait_ge(loaded, n_loads)
                for n, w in enumerate((wq, wk, wv)):
                    for h in range(HEADS):
                        bank = (n * 2 + h // 4)
                        last = nc.tensor.transpose(ps[bank][0:D, (h % 4) * 128:(h % 4 + 1) * 128],
                                                   w[:, h:h + (D - 1) * HEADS + 1:HEADS], P["ident"][:, :])
                last.then_inc(wt, 1)
                pe.wait_ge(wc, 6)
                for h in range(HEADS):
                    last = nc.tensor.matmul(ps[6][:, h * D:(h + 1) * D], turned[0][:, h * 128:(h + 1) * 128],
                                            turned[1][:, h * 128:h * 128 + D], start=True, stop=True)
                for h in range(HEADS):
                    s, k = h % 2, h // 2
                    last = nc.tensor.matmul(ps[7][s * D:(s + 1) * D, k * D:(k + 1) * D],
                                            turned[2][:, h * 128:h * 128 + D], wo[:, h * D:(h + 1) * D],
                                            start=True, stop=True)
                last.then_inc(folded, 1)

            @block.scalar
            def _(act):
                act.wait_ge(wt, 1)
                for n in range(6):
                    nc.scalar.activation(turned[n // 2][:, (n % 2) * 512:(n % 2 + 1) * 512], ps[n][0:D, :],
                                         ACT.Copy).then_inc(wc, 1)

            @block.vector
            def _(dve):
                dve.wait_ge(zeroed, 3)
                dve.wait_ge(loaded, n_loads)
                nc.vector.tensor_copy(cpad[:, T - D:T], backwards(taps[:, :])).then_inc(reversed_taps, 1)
                count = [0]

                def done(ins):
                    count[0] += 1
                    ins.then_inc(split, 1)

                def both(high, low, src):
                    done(nc.vector.tensor_copy(high, src))
                    dve.wait_ge(split, count[0])
                    done(nc.vector.tensor_tensor(low, src, high.bitcast(F32), ALU.subtract))

                both(P["up_high"][:, :], P["up_low"][:, :], up[:, :])
                both(P["router"][:, 0:NE], P["router"][:, NE:2 * NE], router[:, :])
                both(P["up2_high"][:, :], P["up2_low"][:, :], up2[:, :])
                both(P["down2_high"][:, :], P["down2_low"][:, :], down2[:, :])
                done(nc.vector.tensor_copy(P["gate2"][:, :], zeros[:, 0:HC * 128]))
                dve.wait_ge(split, count[0])
                for k in range(HC):
                    both(P["gate2"][:, k * 128:k * 128 + NE], P["gate2"][:, k * 128 + NE:k * 128 + 2 * NE],
                         gate2[:, k * NE:(k + 1) * NE])
                done(nc.vector.tensor_copy(P["ones"][:, :], ones[0:33, 0:T]))
                done(nc.vector.tensor_copy(P["down2_bias"][:, :], zeros[0:33, :]))
                dve.wait_ge(split, count[0])
                done(nc.vector.tensor_copy(P["down2_bias"][0:1, :], bias_row[:, :]))
                dve.wait_ge(split, count[0])
                done(nc.vector.tensor_tensor(bias_low[:, :], bias_row[:, :], P["down2_bias"][0:1, :].bitcast(F32),
                                             ALU.subtract))
                dve.wait_ge(split, count[0])
                done(nc.vector.tensor_copy(P["down2_bias"][32:33, :], bias_low[:, :]))
                done(nc.vector.tensor_copy(P["sel"][:, :], sel_raw[:, :]))
                dve.wait_ge(folded, 1)
                done(nc.vector.tensor_copy(fold[:, :], ps[6][:, :]))
                dve.wait_ge(split, count[0])
                both(P["score_high"][:, :], P["score_low"][:, :], fold[:, :])
                done(nc.vector.tensor_copy(P["value"][:, :], ps[7][:, 0:CH * D]))



def tokens(nc, sb, pb, sem, A, P):
    CB = 16
    NC = B // CB
    R = 4 * G8
    MAPS = NMAP * G8
    with ExitStack() as tmp:
        def scratch(name, shape, dt=F32):
            return tmp.enter_context(nc.sbuf_tensor(name, shape, dt))

        x = scratch("image", [IMG, B * IMG])
        rows = scratch("row_filters", [IMG, R])
        cols = scratch("col_filters", [IMG, 4 * MAPS])
        z = scratch("row_filtered", [IMG, 4 * B * G8])
        maps = scratch("maps", [MAPS + 1, B * G8])
        proj = scratch("projection", [MAPS + 1, G8 * D])
        tok = [scratch(f"token_tile{i}", [128, G8 * D]) for i in range(2)]
        ps = [pb(f"tok_ps{i}", [128, 512]) for i in range(8)]
        filters = sem("filters_loaded")
        images = [sem(f"image_loaded{k}") for k in range(NC)]
        cleared = sem("projection_cleared")
        projection = sem("projection_loaded")
        filtered = sem("rows_filtered")
        copied = sem("rows_copied")
        mapped = sem("maps_ready")
        kept = sem("maps_copied")
        projected = sem("tokens_projected")
        evacuated = sem("tokens_copied")
        stored = [sem(f"tokens_stored{i}") for i in range(2)]
        arrived = sem("tokens_arrived")
        zv = z[:, :].rearrange("p (r n) -> p r n", r=4)

        with nc.Block() as block:
            @block.sync
            def _(sp):
                sp.dma_start(rows[:, :], A["c_rows"]).then_inc(filters, 16)
                sp.dma_start(cols[:, :], A["c_cols"]).then_inc(filters, 16)
                for k in range(NC):
                    sp.dma_start(x[:, k * CB * IMG:(k + 1) * CB * IMG].rearrange("p (b c) -> p b c", b=CB),
                                 A["x"][k * CB:(k + 1) * CB, 0].rearrange("b r c -> r b c")).then_inc(images[k], 16)
                sp.dma_start(halves(P["h"][TI:T, :], B), A["txt"].rearrange("b t d -> t b d")).then_inc(arrived, 16)
                for k in range(NC):
                    sp.wait_ge(evacuated, k + 1)
                    sp.dma_start(P["tok_dram"][k * CB:(k + 1) * CB].rearrange("b (i j) d -> (b i) (j d)", j=G8),
                                 tok[k % 2][:, :]).then_inc(stored[k % 2], 16)
                    if k % 2:
                        for s in stored:
                            sp.wait_ge(s, 8 * (k + 1))
                        n = 2 * CB
                        b0 = (k - 1) * CB
                        sp.dma_start(halves(P["h"][0:TI, b0 * D:(b0 + n) * D], n),
                                     P["tok_dram"][b0:b0 + n].rearrange("b t d -> t b d")).then_inc(arrived, 16)
                sp.wait_ge(arrived, 16 * (1 + NC // 2))

            @block.gpsimd
            def _(pool):
                nc.gpsimd.memset(proj[:, :], 0.0).then_inc(cleared, 1)
                nc.gpsimd.memset(maps[:, :], 1.0).then_inc(cleared, 1)
                pool.wait_ge(cleared, 2)
                for j in range(G8):
                    pool.dma_start(proj[j:j + (NMAP - 1) * G8 + 1:G8, j * D:(j + 1) * D],
                                   A["L0_tok_W"]).then_inc(projection, 16)
                    pool.dma_start(proj[MAPS:MAPS + 1, j * D:(j + 1) * D],
                                   A["L0_tok_b"].unsqueeze(0)).then_inc(projection, 16)
                pool.wait_ge(projection, 2 * G8 * 16)

            @block.tensor
            def _(pe):
                pe.wait_ge(filters, 32)
                for k in range(NC):
                    pe.wait_ge(images[k], 16)
                    if k >= 4:
                        pe.wait_ge(copied, k - 3)
                    for b in range(CB):
                        at = (k * CB + b) * IMG
                        last = nc.tensor.matmul(ps[k % 4][0:IMG, b * R:(b + 1) * R], x[:, at:at + IMG],
                                                rows[:, :], start=True, stop=True)
                    last.then_inc(filtered, 1)
                for n in range(B * G8 // 512):
                    pe.wait_ge(copied, 4 * n + 4)
                    for r in range(4):
                        last = nc.tensor.matmul(ps[4 + n][0:MAPS, :], cols[:, r * MAPS:(r + 1) * MAPS],
                                                z[:, r * B * G8 + n * 512:r * B * G8 + (n + 1) * 512],
                                                start=(r == 0), stop=(r == 3))
                    last.then_inc(mapped, 1)
                pe.wait_ge(projection, 2 * G8 * 16)
                for k in range(NC):
                    pe.wait_ge(kept, k // 4 + 1)
                    if k >= 2:
                        pe.wait_ge(evacuated, k - 1)
                    nc.tensor.matmul(ps[6 + k % 2][:, :], maps[:, k * 128:(k + 1) * 128], proj[:, :],
                                     start=True, stop=True).then_inc(projected, 1)

            @block.vector
            def _(dve):
                dve.wait_ge(cleared, 2)
                for k in range(NC):
                    dve.wait_ge(filtered, k + 1)
                    nc.vector.tensor_copy(
                        zv[:, :, k * CB * G8:(k + 1) * CB * G8].rearrange("p r (b i) -> p r b i", i=G8),
                        ps[k % 4][0:IMG, :].rearrange("p (b r i) -> p r b i", r=4, i=G8)).then_inc(copied, 1)
                for n in range(B * G8 // 512):
                    dve.wait_ge(mapped, n + 1)
                    nc.vector.tensor_copy(maps[0:MAPS, n * 512:(n + 1) * 512], ps[4 + n][0:MAPS, :]).then_inc(kept, 1)

            @block.scalar
            def _(act):
                for k in range(NC):
                    act.wait_ge(projected, k + 1)
                    if k >= 2:
                        act.wait_ge(stored[k % 2], 16 * (k // 2))
                    nc.scalar.activation(tok[k % 2][:, :], ps[6 + k % 2][:, :], ACT.Copy).then_inc(evacuated, 1)



def convolution(nc, sb, pb, sem, A, P):
    QC = 4
    with ExitStack() as tmp:
        def scratch(name, shape, dt=F32):
            return tmp.enter_context(nc.sbuf_tensor(name, shape, dt))

        toeplitz = scratch("toeplitz", [T, D * T])
        u = scratch("conv_in", [T, D * B])
        L = Norm(scratch, sem, "ln1", LB)
        ps = [pb(f"conv_ps{i}", [T, 512]) for i in range(8)]
        CD = D // 4
        hankel = [scratch(f"hankel{i}", [T, CD * T]) for i in range(2)]
        taps = [sem(f"hankel_loaded{i}") for i in range(2)]
        reversed_rows = sem("toeplitz_ready")
        by_channel = lambda t: t.rearrange("p (d t) -> p d t", t=T)
        convolved = sem("convolved")
        added = sem("conv_added")
        uv = u[:, :].rearrange("p (d b) -> p b d", b=B)
        hv = P["h"][:, :].rearrange("p (b d) -> p d b", d=D)
        hb = halves(P["h"][:, :], B)

        with nc.Block() as block:
            @block.sync
            def _(sp):
                pad = P["cpad_dram"]
                for k in range(4):
                    if k >= 2:
                        sp.wait_ge(reversed_rows, k - 1)
                    src = bass.AP(tensor=pad.tensor, offset=pad.offset + k * CD * 2 * T,
                                  ap=[[1, T], [2 * T, CD], [1, T]])
                    sp.dma_start(by_channel(hankel[k % 2][:, :]), src).then_inc(taps[k % 2], 16)
                for s in taps:
                    sp.wait_ge(s, 32)

            @block.vector
            def _(dve):
                group = lambda t: hb[:, t * LB:(t + 1) * LB, :]
                for t in range(NLG + 1):
                    if t < NLG:
                        norm_sum(nc, dve, L, group(t), t % 2)
                        norm_centre(nc, dve, L, group(t), t, t % 2)
                    if t:
                        norm_scale(nc, dve, L, uv[:, (t - 1) * LB:t * LB, :], t - 1, (t - 1) % 2)
                    if t < NLG:
                        norm_power(nc, dve, L, t, t % 2)
                for n in range(D // QC):
                    dve.wait_ge(convolved, n + 1)
                    at = hv[:, n * QC:(n + 1) * QC, :]
                    nc.vector.tensor_tensor(at, at, ps[n % 8][:, :].rearrange("p (c b) -> p c b", c=QC),
                                            ALU.add).then_inc(added, 1)

            @block.scalar
            def _(act):
                for t in range(NLG):
                    norm_square(nc, act, L, t, t % 2)
                    if t < 4:
                        act.wait_ge(taps[t % 2], 16 * (t // 2 + 1))
                        nc.scalar.activation(by_channel(toeplitz[:, t * CD * T:(t + 1) * CD * T]),
                                             backwards(by_channel(hankel[t % 2][:, :])),
                                             ACT.Copy).then_inc(reversed_rows, 1)

            @block.gpsimd
            def _(pool):
                for t in range(NLG):
                    norm_rstd(nc, pool, L, P["norm_consts"], t, t % 2)

            @block.tensor
            def _(pe):
                pe.wait_ge(reversed_rows, 4)
                pe.wait_ge(L.normed, NLG)
                for n in range(D // QC):
                    if n >= 8:
                        pe.wait_ge(added, n - 7)
                    for c in range(QC):
                        d = n * QC + c
                        last = nc.tensor.matmul(ps[n % 8][:, c * B:(c + 1) * B], toeplitz[:, d * T:(d + 1) * T],
                                                u[:, d * B:(d + 1) * B], start=True, stop=True)
                    last.then_inc(convolved, 1)



def first_argmax(nc, step, probs, rank, top, ties, out, shape):
    p, n = shape
    step(nc.vector.tensor_reduce(top, probs, axis=AX_X, op=ALU.max))
    step(nc.vector.tensor_tensor(ties, probs, over(top, NE), ALU.is_equal))
    step(nc.vector.tensor_tensor(ties, ties, rank.unsqueeze(1).to_broadcast([p, n, NE]), ALU.mult))
    step(nc.vector.tensor_reduce(top, ties, axis=AX_X, op=ALU.max))
    step(nc.vector.tensor_tensor(out, ties, over(top, NE), ALU.is_equal))


def route(nc, sb, pb, sem, A, P):
    RB = 8
    NRG = B // RB
    BPB = GB
    NBK = RB // BPB
    with ExitStack() as kept, ExitStack() as tmp:
        logits = kept.enter_context(nc.sbuf_tensor("logits", [T, B * NE], F32))

        def scratch(name, shape, dt=F32):
            return tmp.enter_context(nc.sbuf_tensor(name, shape, dt))

        L = Norm(scratch, sem, "ln2", RB)
        S = Split(scratch, sem, "ln2", RB)
        xn = [scratch(f"ln2_out{i}", [T, RB * D]) for i in range(2)]
        xs = [scratch(f"ln2_stack{i}", [128, RB * T], F32R) for i in range(2)]
        ps_turn = [pb(f"route_turn{i}", [128, 512]) for i in range(4)]
        ps_logit = [pb(f"route_logit{i}", [128, 512]) for i in range(2)]
        scored = sem("router_scored")
        gathered = sem("logits_ready")
        residual = sem("norm_added")
        stacked = [sem(f"stack_stored{i}") for i in range(2)]
        hb = halves(P["h"][:, :], B)
        lg = logits[:, :].rearrange("p (b e) -> p b e", e=NE)

        with nc.Block() as block:
            @block.vector
            def _(dve):
                group = lambda t: hb[:, t * RB:(t + 1) * RB, :]

                def collect(t):
                    dve.wait_ge(scored, t + 1)
                    nc.vector.tensor_reduce(
                        lg[:, t * RB:(t + 1) * RB, :],
                        ps_logit[t % 2][0:T, 0:RB * 2 * NE].rearrange("p (b two e) -> p b e two", two=2, e=NE),
                        axis=AX_X, op=ALU.add).then_inc(gathered, 1)

                for t in range(NRG + 2):
                    if t < NRG:
                        norm_sum(nc, dve, L, group(t), t % 2)
                        norm_centre(nc, dve, L, group(t), t, t % 2)
                    if 1 <= t <= NRG:
                        if t >= 3:
                            dve.wait_ge(residual, t - 2)
                        norm_scale(nc, dve, L, halves(xn[(t - 1) % 2][:, :], RB), t - 1, (t - 1) % 2)
                    if t < NRG:
                        norm_power(nc, dve, L, t, t % 2)
                    if 1 <= t <= NRG:
                        split_low(nc, dve, S, halves(xn[(t - 1) % 2][:, :], RB), t - 1, (t - 1) % 2)
                    if t >= 2:
                        collect(t - 2)

            @block.scalar
            def _(act):
                def evacuate(t):
                    if t >= 2:
                        act.wait_ge(scored, t - 1)
                        act.wait_ge(stacked[t % 2], 16 * (t // 2))
                    for k in range(NBK):
                        act.wait_ge(S.turned, t * NBK + k + 1)
                        nc.scalar.activation(xs[t % 2][:, k * GT:(k + 1) * GT], ps_turn[k][:, 0:GT],
                                             ACT.Copy).then_inc(S.stored, 1)

                for t in range(NRG + 2):
                    if t < NRG:
                        norm_square(nc, act, L, t, t % 2)
                    if 1 <= t <= NRG:
                        if t >= 3:
                            act.wait_ge(S.turned, (t - 2) * NBK)
                        split_high(nc, act, L, S, halves(xn[(t - 1) % 2][:, :], RB), t - 1, (t - 1) % 2)
                    if t >= 2:
                        evacuate(t - 2)

            @block.gpsimd
            def _(pool):
                for t in range(NRG + 1):
                    if t < NRG:
                        norm_rstd(nc, pool, L, P["norm_consts"], t, t % 2)
                    if t:
                        pool.wait_ge(L.normed, t)
                        at = P["h"][:, (t - 1) * RB * D:t * RB * D]
                        nc.gpsimd.tensor_tensor(at, at, xn[(t - 1) % 2][:, :], ALU.add).then_inc(residual, 1)

            @block.sync
            def _(sp):
                for t in range(NRG):
                    sp.wait_ge(S.stored, (t + 1) * NBK)
                    sp.dma_start(P["xs"][:, t * RB * T:(t + 1) * RB * T].bitcast(F32),
                                 xs[t % 2][:, :].bitcast(F32)).then_inc(stacked[t % 2], 16)
                for s in stacked:
                    sp.wait_ge(s, 8 * NRG)

            @block.tensor
            def _(pe):
                for t in range(NRG):
                    pe.wait_ge(S.low, t + 1)
                    for k in range(NBK):
                        if t:
                            pe.wait_ge(S.stored, (t - 1) * NBK + k + 1)
                        split_turn(nc, pe, S, P["ident"], ps_turn[k], t, t % 2, k * BPB, BPB)
                    pe.wait_ge(S.stored, (t + 1) * NBK)
                    if t >= 2:
                        pe.wait_ge(gathered, t - 1)
                    for b in range(RB):
                        last = nc.tensor.matmul(ps_logit[t % 2][0:T, b * 2 * NE:(b + 1) * 2 * NE],
                                                xs[t % 2][:, b * T:(b + 1) * T], P["router"][:, :],
                                                start=True, stop=True)
                    last.then_inc(scored, 1)

        tmp.close()
        probs = scratch("probs", [T, B * NE])
        ties = scratch("ties", [T, B * NE])
        first = scratch("first", [T, B * NE])
        second = scratch("second", [T, B * NE])
        top = scratch("top", [T, B])
        weight = [scratch(f"weight{i}", [T, B]) for i in range(2)]
        total = scratch("softmax_total", [T, B])
        gates = scratch("gates", [T, B * 2 * NE], F32R)
        turned_gates = scratch("turned_gates", [128, B // 8 * T], F32R)
        gates_stored = sem("gates_stored")
        PER = 8
        step_done = sem("gate_step")
        exps = sem("router_exp")
        gates_turned = sem("gates_turned")
        gates_copied = sem("gates_copied")
        v3 = lambda t: t[:, :].rearrange("p (b e) -> p b e", e=NE)

        with nc.Block() as block:
            @block.vector
            def _(dve):
                n = [0]

                def step(ins):
                    n[0] += 1
                    ins.then_inc(step_done, 1)
                    dve.wait_ge(step_done, n[0])

                step(nc.vector.tensor_reduce(top[:, :], lg, axis=AX_X, op=ALU.max))
                step(nc.vector.tensor_tensor(lg, lg, over(top[:, :], NE), ALU.subtract))
                dve.wait_ge(exps, 1)
                step(nc.vector.tensor_reduce(total[:, :], v3(probs), axis=AX_X, op=ALU.add))
                step(nc.vector.reciprocal(total[:, :], total[:, :]))
                step(nc.vector.tensor_tensor(v3(probs), v3(probs), over(total[:, :], NE), ALU.mult))
                first_argmax(nc, step, v3(probs), P["rank"][:, :], top[:, :], v3(ties), v3(first), (T, B))
                step(nc.vector.tensor_tensor(v3(ties), v3(probs), v3(first), ALU.mult))
                step(nc.vector.tensor_reduce(weight[0][:, :], v3(ties), axis=AX_X, op=ALU.add))
                step(nc.vector.scalar_tensor_tensor(out=ties[:, :], in0=first[:, :], scalar=-2.0, in1=probs[:, :],
                                                    op0=ALU.mult, op1=ALU.add))
                step(nc.vector.tensor_copy(second[:, :], ties[:, :]))
                first_argmax(nc, step, v3(second), P["rank"][:, :], top[:, :], v3(ties), v3(second), (T, B))
                step(nc.vector.tensor_tensor(v3(ties), v3(probs), v3(second), ALU.mult))
                step(nc.vector.tensor_reduce(weight[1][:, :], v3(ties), axis=AX_X, op=ALU.add))
                step(nc.vector.tensor_tensor(total[:, :], weight[0][:, :], weight[1][:, :], ALU.add))
                step(nc.vector.tensor_scalar(total[:, :], total[:, :], 1e-12, None, ALU.max))
                step(nc.vector.reciprocal(total[:, :], total[:, :]))
                step(nc.vector.tensor_tensor(first[:, :], first[:, :], second[:, :], ALU.add))
                step(nc.vector.tensor_tensor(v3(first), v3(first), over(total[:, :], NE), ALU.mult))
                step(nc.vector.tensor_tensor(first[:, :], first[:, :], probs[:, :], ALU.mult))
                gv = gates[:, :].rearrange("p (b two e) -> p b two e", two=2, e=NE)
                step(nc.vector.tensor_copy(gv[:, :, 0, :], v3(first)))
                step(nc.vector.tensor_tensor(gv[:, :, 1, :], v3(first), gv[:, :, 0, :].bitcast(F32), ALU.subtract))

            GATE_STEPS = 2 + 3 + 5 + 2 + 2 + 5 + 2 + 3 + 3 + 2

            @block.scalar
            def _(act):
                act.wait_ge(step_done, 2)
                nc.scalar.activation(probs[:, :], logits[:, :], ACT.Exp).then_inc(exps, 1)
                for k in range(4):
                    act.wait_ge(gates_turned, k + 1)
                    nc.scalar.activation(turned_gates[:, k * GT:(k + 1) * GT], ps_turn[k][:, 0:GT],
                                         ACT.Copy).then_inc(gates_copied, 1)

            @block.tensor
            def _(pe):
                pe.wait_ge(step_done, GATE_STEPS)
                for k in range(4):
                    for m in range(4):
                        at = (k * 4 + m) * PER * 2 * NE
                        last = nc.tensor.transpose(ps_turn[k][:, m * T:(m + 1) * T],
                                                   gates[:, at:at + PER * 2 * NE].bitcast(F32), P["ident"][0:T, 0:T])
                    last.then_inc(gates_turned, 1)

            @block.sync
            def _(sp):
                sp.wait_ge(gates_copied, 4)
                dst = P["gates"].rearrange("r (o m) t -> r o m t", m=PER)
                for m in range(PER):
                    sp.dma_start(dst[:, :, m, :], turned_gates[m * 2 * NE:(m + 1) * 2 * NE, :].bitcast(F32)
                                 .rearrange("r (o t) -> r o t", t=T)).then_inc(gates_stored, 16)
                sp.wait_ge(gates_stored, 16 * PER)



def run_bodies(eng, body, first, last, steady_first, steady_last):
    assert (steady_last - steady_first + 1) % 2 == 0
    for g in range(first, steady_first):
        body(g, g % 2, g)
    with eng.Fori(0, (steady_last - steady_first + 1) // 2) as i:
        for k in range(2):
            body(i * 2 + (steady_first + k), (steady_first + k) % 2, None)
    for g in range(steady_last + 1, last + 1):
        body(g, g % 2, g)


class Half:

    def __init__(self, twice):
        self.twice = twice

    def __mul__(self, k):
        assert k % 2 == 0
        return self.twice * (k // 2)


def nth_of_parity(g, q):
    return Half(g + (2 - q))


def within(edge, shift, low=0):
    return edge is None or low <= edge - shift < NG


def at_least(edge, shift, low):
    return edge is None or edge - shift >= low


def experts(nc, sb, pb, sem, A, P):
    with ExitStack() as tmp:
        def scratch(name, shape, dt=F32):
            return tmp.enter_context(nc.sbuf_tensor(name, shape, dt))

        L = Norm(scratch, sem, "ln3", GB)
        S = Split(scratch, sem, "ln3", GB)
        hidden = scratch("hidden", [128, CH * GT])
        gated = scratch("gated", [128, CH * GT])
        gate = [scratch(f"gate_stage{i}", [2 * NE, GT], F32R) for i in range(2)]
        y = [scratch(f"expert_sum{i}", [128, GT // 2]) for i in range(2)]
        ps_up = [pb(f"ex_up{i}", [128, 512]) for i in range(2)]
        ps_gate = [pb(f"ex_gate{i}", [128, 512]) for i in range(CH)]
        ps_down = pb("ex_down", [128, 512])
        ps_misc = pb("ex_misc", [128, 512])
        upped = sem("ex_upped")
        gate_loaded = [sem(f"ex_gate_loaded{i}") for i in range(2)]
        gate_spread = sem("ex_gate_spread")
        activated = sem("ex_activated")
        gated_ready = sem("ex_gated")
        downed = sem("ex_downed")
        biased = sem("ex_biased")
        copied = sem("ex_copied")
        turned_back = sem("ex_turned_back")
        updated = sem("ex_updated")
        hb = halves(P["h"][:, :], B)
        xb = halves(P["xn"][:, :], B)
        h_at = lambda g: hb[:, bass.ds(g * GB, GB), :]
        xn_at = lambda g: xb[:, bass.ds(g * GB, GB), :]
        cols = lambda t, c: t[:, c * GT:(c + 1) * GT]
        RUN = (0, NG + 4, 6, NG - 1)

        with nc.Block() as block:
            @block.sync
            def _(sp):
                def body(g, q, edge):
                    if not within(edge, 0):
                        return
                    if at_least(edge, 0, 2):
                        sp.wait_ge(biased, g - 1)
                    sp.dma_start(gate[q][:, :].bitcast(F32).rearrange("r (b t) -> r b t", t=T),
                                 P["gates"][:, bass.ds(g * GB, GB), :]).then_inc(gate_loaded[q], 16)
                run_bodies(sp, body, *RUN)

            @block.tensor
            def _(pe):
                def down(g, q, c, edge):
                    pe.wait_ge(gated_ready, g * CH + (c + 1))
                    if c == 0:
                        if at_least(edge, 1, 1):
                            pe.wait_ge(copied, g)
                        for s in range(2):
                            rhs = gate[q][:, :].bitcast(F32).rearrange("p (m s t) -> p m s t", s=2, t=T)[:, :, s, :]
                            last = nc.tensor.matmul(ps_down[s * D:(s + 1) * D, 0:GT // 2], P["down_bias"][:, :], rhs,
                                                    start=True, stop=False)
                        last.then_inc(biased, 1)
                    for s in range(2):
                        rhs = cols(gated, c).rearrange("p (m s t) -> p m s t", s=2, t=T)[:, :, s, :]
                        last = nc.tensor.matmul(ps_down[s * D:(s + 1) * D, 0:GT // 2],
                                                P["down"][:, c * D:(c + 1) * D], rhs, start=False, stop=(c == CH - 1))
                    last.then_inc(downed, 1)

                def body(g, q, edge):
                    for c in range(CH):
                        if within(edge, 1):
                            down(g - 1, 1 - q, c, edge)
                        if within(edge, 0):
                            n = g * CH + c
                            if edge is None or edge * CH + c >= 2:
                                pe.wait_ge(activated, n - 1)
                            x = P["xs"][:, bass.ds(g * GT, GT)]
                            nc.tensor.matmul(ps_up[c % 2][:, 0:GT], P["up_high"][:, c * 128:(c + 1) * 128], x,
                                             start=True, stop=False)
                            nc.tensor.matmul(ps_up[c % 2][:, 0:GT], P["up_low"][:, c * 128:(c + 1) * 128], x,
                                             start=False, stop=True).then_inc(upped, 1)
                            if c == 0:
                                pe.wait_ge(gate_loaded[q], nth_of_parity(g, q) * 16)
                            if at_least(edge, 0, 1):
                                pe.wait_ge(gated_ready, n - (CH - 1))
                            nc.tensor.matmul(ps_gate[c][:, 0:GT], P["sel"][:, c * 128:(c + 1) * 128],
                                             gate[q][:, :], start=True, stop=True).then_inc(gate_spread, 1)
                        if c == 0 and within(edge, 5):
                            pe.wait_ge(S.low, g - 4)
                            if within(edge, 3):
                                pe.wait_ge(updated, g - 2)
                            else:
                                pe.wait_ge(S.stored, g - 5)
                            split_turn(nc, pe, S, P["ident"], ps_misc, g - 5, 1 - q, 0, GB)
                        if c == 2 and within(edge, 2):
                            pe.wait_ge(copied, g - 1)
                            if at_least(edge, 5, 0):
                                pe.wait_ge(S.stored, g - 4)
                            elif at_least(edge, 3, 0):
                                pe.wait_ge(updated, g - 2)
                            for m in range(GB // 2):
                                last = nc.tensor.transpose(ps_misc[0:T, m * 128:(m + 1) * 128],
                                                           y[q][:, m * T:(m + 1) * T], P["ident"][:, :])
                            last.then_inc(turned_back, 1)
                run_bodies(pe, body, *RUN)

            @block.scalar
            def _(act):
                def body(g, q, edge):
                    for c in range(CH):
                        if c == 3 and within(edge, 1):
                            act.wait_ge(downed, g * CH)
                            if at_least(edge, 1, 2):
                                act.wait_ge(turned_back, g - 2)
                            nc.scalar.activation(y[1 - q][:, :], ps_down[:, 0:GT // 2], ACT.Copy).then_inc(copied, 1)
                        if within(edge, 0):
                            n = g * CH + c
                            act.wait_ge(upped, n + 1)
                            if at_least(edge, 0, 1):
                                act.wait_ge(gated_ready, n - 3)
                            nc.scalar.activation(cols(hidden, c), ps_up[c % 2][:, 0:GT], ACT.Gelu,
                                                 bias=P["up_bias"][:, c:c + 1]).then_inc(activated, 1)
                        if c == 0 and within(edge, 4):
                            split_high(nc, act, L, S, xn_at(g - 4), g - 4, q)
                        if c == 0 and within(edge, 3):
                            norm_square(nc, act, L, g - 3, 1 - q)
                        if c == 1 and within(edge, 5):
                            act.wait_ge(S.turned, g - 4)
                            nc.scalar.activation(P["xs"][:, bass.ds((g - 5) * GT, GT)], ps_misc[:, 0:GT],
                                                 ACT.Copy).then_inc(S.stored, 1)
                run_bodies(act, body, *RUN)

            @block.vector
            def _(dve):
                def gate_chunk(g, c, edge):
                    n = g * CH + c
                    dve.wait_ge(activated, n + 1)
                    dve.wait_ge(gate_spread, n + 1)
                    if at_least(edge, 0, 1):
                        dve.wait_ge(downed, n - (CH - 1))
                    nc.vector.tensor_tensor(cols(gated, c), cols(hidden, c), ps_gate[c][:, 0:GT],
                                            ALU.mult).then_inc(gated_ready, 1)

                def body(g, q, edge):
                    main, summed, scaled, split = (within(edge, s) for s in (0, 2, 3, 4))
                    if main:
                        gate_chunk(g, 0, edge)
                    if split:
                        split_low(nc, dve, S, xn_at(g - 4), g - 4, q)
                    if main:
                        gate_chunk(g, 1, edge)
                    if scaled:
                        norm_power(nc, dve, L, g - 3, 1 - q)
                    if main:
                        gate_chunk(g, 2, edge)
                    if summed:
                        dve.wait_ge(turned_back, g - 1)
                        nc.vector.tensor_tensor(h_at(g - 2), h_at(g - 2),
                                                ps_misc[0:T, 0:GB * D].rearrange("p (b x) -> p b x", b=GB),
                                                ALU.add).then_inc(updated, 1)
                        dve.wait_ge(updated, g - 1)
                    if main:
                        gate_chunk(g, 3, edge)
                    if summed:
                        norm_sum(nc, dve, L, h_at(g - 2), q)
                    if scaled:
                        norm_scale(nc, dve, L, xn_at(g - 3), g - 3, 1 - q)
                    if summed:
                        norm_centre(nc, dve, L, h_at(g - 2), g - 2, q)
                run_bodies(dve, body, *RUN)

            @block.gpsimd
            def _(pool):
                def body(g, q, edge):
                    if within(edge, 3):
                        norm_rstd(nc, pool, L, P["norm_consts"], g - 3, 1 - q)
                run_bodies(pool, body, *RUN)


def attention(nc, sb, pb, sem, A, P):
    with ExitStack() as tmp:
        def scratch(name, shape, dt=F32):
            return tmp.enter_context(nc.sbuf_tensor(name, shape, dt))

        L = Norm(scratch, sem, "ln4", GB)
        S = Split(scratch, sem, "ln4", GB)
        xn = [scratch(f"ln4_out{i}", [T, GB * D]) for i in range(2)]
        xh = [scratch(f"x_high{i}", [128, GT], F32R) for i in range(2)]
        xl = [scratch(f"x_low{i}", [128, GT], F32R) for i in range(2)]
        xt = [scratch(f"x_tokens{i}", [T, GB * D]) for i in range(2)]
        mh = [scratch(f"xm_high{i}", [128, CH * GT], F32R) for i in range(2)]
        ml = [scratch(f"xm_low{i}", [128, CH * GT], F32R) for i in range(2)]
        attn = [scratch(f"attn{i}", [T, HEADS * T]) for i in range(2)]
        ax = [scratch(f"attn_x{i}", [128, GB * CH * T]) for i in range(2)]
        y = [scratch(f"attn_sum{i}", [128, GT // 2]) for i in range(2)]
        ps_m = [pb(f"at_xm{i}", [128, 512]) for i in range(2)]
        ps_s = [pb(f"at_scores{i}", [128, 1024]) for i in range(2)]
        ps_x = pb("at_ax", [128, 512])
        ps_misc = pb("at_misc", [128, 512])
        staged = [sem(f"at_staged{i}") for i in range(2)]
        projected = sem("at_xm")
        high = sem("at_xm_high")
        low = sem("at_xm_low")
        scored = sem("at_scored")
        weighed = sem("at_weighed")
        applied = sem("at_applied")
        kept = sem("at_kept")
        summed = sem("at_summed")
        copied = sem("at_copied")
        turned_back = sem("at_turned_back")
        updated = sem("at_updated")
        hb = halves(P["h"][:, :], B)
        xb = halves(P["xn"][:, :], B)
        h_at = lambda g: hb[:, bass.ds(g * GB, GB), :]
        cols = lambda t, c: t[:, c * GT:(c + 1) * GT]
        RUN = (-1, NG + 3, 5, NG - 2)
        SEM = float(D) ** 0.5
        STAGED = 5 * 16

        with nc.Block() as block:
            @block.sync
            def _(sp):
                def body(g, q, edge):
                    if not within(edge, 0):
                        return
                    if at_least(edge, 0, 2):
                        sp.wait_ge(scored, g * GB - GB)
                        sp.wait_ge(applied, g * GB - GB)
                    for s in range(2):
                        at = slice(s * D, (s + 1) * D)
                        for half, x in enumerate((xh, xl)):
                            sp.dma_start(x[q][at, :].bitcast(F32),
                                         P["xs"][half * D:(half + 1) * D, bass.ds(g * GT, GT)].bitcast(F32)
                                         ).then_inc(staged[q], 16)
                    sp.dma_start(xt[q][:, :], P["xn"][:, bass.ds(g * GB * D, GB * D)]).then_inc(staged[q], 16)
                run_bodies(sp, body, *RUN)

            @block.tensor
            def _(pe):
                def scores(g, q, b, edge):
                    n = g * GB + b
                    if b == 0:
                        pe.wait_ge(low, (g + 1) * CH)
                        pe.wait_ge(staged[q], nth_of_parity(g, q) * STAGED)
                    if edge is None or edge * GB + b >= 2:
                        pe.wait_ge(weighed, n - 1)
                    for s in range(2):
                        at = slice(s * D, (s + 1) * D)
                        out = ps_s[b % 2][0:T, s * 512:s * 512 + CH * T]
                        mv = lambda t: t[at, :].rearrange("p (k b t) -> p k b t", k=CH, b=GB)[:, :, b, :]
                        tb = slice(b * T, (b + 1) * T)
                        nc.tensor.matmul(out, xh[q][at, tb], mv(mh[q]), start=True, stop=False)
                        nc.tensor.matmul(out, xh[q][at, tb], mv(ml[q]), start=False, stop=False)
                        last = nc.tensor.matmul(out, xl[q][at, tb], mv(mh[q]), start=False, stop=True)
                    last.then_inc(scored, 1)

                def project(g, k, edge):
                    if edge is None or (edge + 1) * CH + k >= 2:
                        pe.wait_ge(low, g * CH + (k - 1))
                    x = P["xs"][:, bass.ds(g * GT, GT)]
                    nc.tensor.matmul(ps_m[k % 2][:, 0:GT], P["score_high"][:, k * 128:(k + 1) * 128], x,
                                     start=True, stop=False)
                    nc.tensor.matmul(ps_m[k % 2][:, 0:GT], P["score_low"][:, k * 128:(k + 1) * 128], x,
                                     start=False, stop=True).then_inc(projected, 1)

                def apply(g, q, b, edge, shift):
                    n = g * GB + b
                    pe.wait_ge(weighed, n + 1)
                    if edge is None or (edge - shift) * GB + b >= 1:
                        pe.wait_ge(kept, n)
                    for s in range(2):
                        last = nc.tensor.matmul(ps_x[s * D:(s + 1) * D, 0:CH * T], xt[q][:, b * D:(b + 1) * D],
                                                attn[b % 2][:, s * CH * T:(s + 1) * CH * T], start=True, stop=True)
                    last.then_inc(applied, 1)

                def body(g, q, edge):
                    for b in range(GB):
                        if within(edge, 0):
                            scores(g, q, b, edge)
                        if within(edge, -1):
                            project(g + 1, b, edge)
                        if b == 0 and within(edge, 1):
                            apply(g - 1, 1 - q, GB - 1, edge, 1)
                        if b and within(edge, 0):
                            apply(g, q, b - 1, edge, 0)
                        if b == 0 and within(edge, 4):
                            pe.wait_ge(S.low, g - 3)
                            pe.wait_ge(updated, g - 1 if edge is None else min(g - 1, NG))
                            if edge is not None and edge - 2 >= NG:
                                pe.wait_ge(S.stored, g - 4)
                            split_turn(nc, pe, S, P["ident"], ps_misc, g - 4, q, 0, GB)
                        if b == 1 and within(edge, 1):
                            pe.wait_ge(kept, g * GB)
                            if at_least(edge, 4, 0):
                                pe.wait_ge(S.stored, g - 3)
                            elif at_least(edge, 2, 0):
                                pe.wait_ge(updated, g - 1)
                            for s in range(2):
                                for k in range(CH):
                                    rhs = ax[1 - q][:, :].rearrange("p (m s k t) -> p m s k t", s=2, k=CH,
                                                                    t=T)[:, :, s, k, :]
                                    last = nc.tensor.matmul(ps_misc[s * D:(s + 1) * D, 0:GT // 2],
                                                            P["value"][:, k * D:(k + 1) * D], rhs,
                                                            start=(k == 0), stop=(k == CH - 1))
                            last.then_inc(summed, 1)
                        if b == 3 and within(edge, 1):
                            pe.wait_ge(copied, g)
                            for m in range(GB // 2):
                                last = nc.tensor.transpose(ps_misc[0:T, m * 128:(m + 1) * 128],
                                                           y[1 - q][:, m * T:(m + 1) * T], P["ident"][:, :])
                            last.then_inc(turned_back, 1)
                run_bodies(pe, body, *RUN)

            @block.scalar
            def _(act):
                def body(g, q, edge):
                    for b in range(GB):
                        if within(edge, -1):
                            n = (g + 1) * CH + b
                            act.wait_ge(projected, n + 1)
                            if at_least(edge, -1, 2):
                                act.wait_ge(scored, g * GB)
                            nc.scalar.activation(cols(mh[1 - q], b), ps_m[b % 2][:, 0:GT],
                                                 ACT.Copy).then_inc(high, 1)
                        if within(edge, 0):
                            n = g * GB + b
                            act.wait_ge(scored, n + 1)
                            if edge is None or edge * GB + b >= 2:
                                act.wait_ge(applied, n - 1)
                            nc.scalar.activation(
                                attn[b % 2][:, :].rearrange("p (s n) -> p s n", s=2),
                                ps_s[b % 2][0:T, :].rearrange("p (s n) -> p s n", s=2)[:, :, 0:CH * T],
                                ACT.Sigmoid, scale=SEM).then_inc(weighed, 1)
                        if b == 1 and within(edge, 2):
                            norm_square(nc, act, L, g - 2, q)
                        if b == 0 and within(edge, 4):
                            act.wait_ge(S.turned, g - 3)
                            nc.scalar.activation(P["xs"][:, bass.ds((g - 4) * GT, GT)], ps_misc[:, 0:GT],
                                                 ACT.Copy).then_inc(S.stored, 1)
                        if b == 0 and within(edge, 3):
                            split_high(nc, act, L, S, halves(xn[1 - q][:, :], GB), g - 3, 1 - q)
                run_bodies(act, body, *RUN)

            @block.vector
            def _(dve):
                def rest(g, q, k):
                    dve.wait_ge(high, g * CH + (k + 1))
                    nc.vector.tensor_tensor(cols(ml[q], k), ps_m[k % 2][:, 0:GT], cols(mh[q], k).bitcast(F32),
                                            ALU.subtract).then_inc(low, 1)

                def keep(g, q, b):
                    dve.wait_ge(applied, g * GB + (b + 1))
                    nc.vector.tensor_copy(ax[q][:, b * CH * T:(b + 1) * CH * T],
                                          ps_x[:, 0:CH * T]).then_inc(kept, 1)

                def body(g, q, edge):
                    ahead, main, mid, tail, last = (within(edge, s) for s in (-1, 0, 1, 2, 3))
                    if last:
                        norm_scale(nc, dve, L, halves(xn[1 - q][:, :], GB), g - 3, 1 - q)
                    if tail:
                        dve.wait_ge(updated, g - 1)
                    if ahead:
                        rest(g + 1, 1 - q, 0)
                    if mid:
                        keep(g - 1, 1 - q, GB - 1)
                    if tail:
                        norm_sum(nc, dve, L, h_at(g - 2), q)
                    if last:
                        split_low(nc, dve, S, halves(xn[1 - q][:, :], GB), g - 3, 1 - q)
                    if ahead:
                        rest(g + 1, 1 - q, 1)
                    if tail:
                        norm_centre(nc, dve, L, h_at(g - 2), g - 2, q)
                    if main:
                        keep(g, q, 0)
                    if mid:
                        dve.wait_ge(summed, g)
                        nc.vector.tensor_copy(y[1 - q][:, :], ps_misc[:, 0:GT // 2]).then_inc(copied, 1)
                    if ahead:
                        rest(g + 1, 1 - q, 2)
                    if main:
                        keep(g, q, 1)
                    if tail:
                        norm_power(nc, dve, L, g - 2, q)
                    if ahead:
                        rest(g + 1, 1 - q, 3)
                    if main:
                        keep(g, q, 2)
                    if mid:
                        dve.wait_ge(turned_back, g)
                        nc.vector.scalar_tensor_tensor(
                            out=h_at(g - 1), in0=ps_misc[0:T, 0:GB * D].rearrange("p (b x) -> p b x", b=GB),
                            scalar=0.0, in1=h_at(g - 1), op0=ALU.max, op1=ALU.add).then_inc(updated, 1)
                run_bodies(dve, body, *RUN)

            @block.gpsimd
            def _(pool):
                def body(g, q, edge):
                    if within(edge, 2):
                        norm_rstd(nc, pool, L, P["norm_consts"], g - 2, q)
                run_bodies(pool, body, *RUN)


def last_layer(nc, sb, pb, sem, A, P):
    with ExitStack() as tmp:
        def scratch(name, shape, dt=F32):
            return tmp.enter_context(nc.sbuf_tensor(name, shape, dt))

        hidden = scratch("hidden2", [128, HC * GT])
        hh = [scratch(f"hidden_high{i}", [128, HC * GT], F32R) for i in range(2)]
        hl = [scratch(f"hidden_low{i}", [128, HC * GT], F32R) for i in range(2)]
        lt = scratch("logits_turned", [128, GT])
        logits = scratch("logits2", [T, B * NE])
        small = scratch("logits_now", [T, GB * NE])
        ties = scratch("ties2", [T, GB * NE])
        top = scratch("top2", [T, GB])
        chosen = [scratch(f"chosen{i}", [T, GB * NE]) for i in range(2)]
        picked = [scratch(f"picked{i}", [T, NE * D]) for i in range(2)]
        ps_up = [pb(f"la_up{i}", [128, 512]) for i in range(2)]
        ps_logit = pb("la_logit", [128, 512])
        ps_turn = pb("la_turn", [128, 512])
        ps_y = [pb(f"la_y{i}", [128, 512]) for i in range(4)]
        upped = sem("la_upped")
        activated = sem("la_activated")
        high = sem("la_high")
        low = sem("la_low")
        scored = sem("la_scored")
        logit_copied = sem("la_logit_copied")
        logit_turned = sem("la_logit_turned")
        choice_step = sem("la_choice_step")
        downed = sem("la_downed")
        masked = sem("la_masked")
        reduced = sem("la_reduced")
        lg_all = logits[:, :].rearrange("p (b e) -> p b e", e=NE)
        cols = lambda t, c: t[:, c * GT:(c + 1) * GT]
        v3 = lambda t: t[:, :].rearrange("p (b e) -> p b e", e=NE)
        STEPS = 7
        RUN = (-1, NG - 1, 1, NG - 2)

        with nc.Block() as block:
            @block.tensor
            def _(pe):
                def down(g, q, b, edge):
                    n = g * GB + b
                    if b == 0:
                        pe.wait_ge(low, (g + 1) * HC)
                    if at_least(edge, 0, 1):
                        pe.wait_ge(masked, n - 3)
                    out = ps_y[b][0:T, :]
                    tb = lambda c: slice(c * GT + b * T, c * GT + (b + 1) * T)
                    wc = lambda c: slice(c * 512, (c + 1) * 512)
                    nc.tensor.matmul(out, P["ones"][:, :], P["down2_bias"][:, :], start=True, stop=False)
                    for c in range(HC):
                        nc.tensor.matmul(out, hh[q][:, tb(c)], P["down2_high"][:, wc(c)], start=False, stop=False)
                        nc.tensor.matmul(out, hh[q][:, tb(c)], P["down2_low"][:, wc(c)], start=False, stop=False)
                        last = nc.tensor.matmul(out, hl[q][:, tb(c)], P["down2_high"][:, wc(c)], start=False,
                                                stop=(c == HC - 1))
                    last.then_inc(downed, 1)

                def body(g, q, edge):
                    ahead = within(edge, -1)
                    if ahead:
                        for c in range(HC):
                            if at_least(edge, -1, 1):
                                pe.wait_ge(activated, g * HC + (c + 1))
                            x = P["xs"][:, bass.ds((g + 1) * GT, GT)]
                            nc.tensor.matmul(ps_up[c][:, 0:GT], P["up2_high"][:, c * 128:(c + 1) * 128], x,
                                             start=True, stop=False)
                            nc.tensor.matmul(ps_up[c][:, 0:GT], P["up2_low"][:, c * 128:(c + 1) * 128], x,
                                             start=False, stop=True).then_inc(upped, 1)
                    if within(edge, 0):
                        down(g, q, 0, edge)
                        down(g, q, 1, edge)
                    if ahead:
                        pe.wait_ge(low, (g + 2) * HC)
                        if at_least(edge, -1, 1):
                            pe.wait_ge(logit_copied, g + 1)
                        for c in range(HC):
                            for h in (hh, hl):
                                last = nc.tensor.matmul(ps_logit[:, 0:GT], P["gate2"][:, c * 128:(c + 1) * 128],
                                                        cols(h[1 - q], c), start=(c == 0 and h is hh),
                                                        stop=(c == HC - 1 and h is hl))
                        last.then_inc(scored, 1)
                    if within(edge, 0):
                        down(g, q, 2, edge)
                    if ahead:
                        pe.wait_ge(logit_copied, g + 2)
                        if at_least(edge, -1, 1):
                            pe.wait_ge(choice_step, (g + 1) * STEPS)
                        for b in range(GB):
                            last = nc.tensor.transpose(ps_turn[0:T, b * 128:(b + 1) * 128],
                                                       lt[:, b * T:(b + 1) * T], P["ident"][:, :])
                        last.then_inc(logit_turned, 1)
                    if within(edge, 0):
                        down(g, q, 3, edge)
                run_bodies(pe, body, *RUN)

            @block.scalar
            def _(act):
                def body(g, q, edge):
                    if not within(edge, -1):
                        return
                    for c in range(HC):
                        act.wait_ge(upped, (g + 1) * HC + (c + 1))
                        if at_least(edge, -1, 1):
                            act.wait_ge(low, g * HC + (c + 1))
                        nc.scalar.activation(cols(hidden, c), ps_up[c][:, 0:GT], ACT.Gelu,
                                             bias=P["up2_bias"][:, c:c + 1]).then_inc(activated, 1)
                    if at_least(edge, -1, 2):
                        act.wait_ge(downed, g * GB)
                    for c in range(HC):
                        act.wait_ge(activated, (g + 1) * HC + (c + 1))
                        nc.scalar.activation(cols(hh[1 - q], c), cols(hidden, c), ACT.Copy).then_inc(high, 1)
                    act.wait_ge(scored, g + 2)
                    if at_least(edge, -1, 1):
                        act.wait_ge(logit_turned, g + 1)
                    nc.scalar.activation(lt[:, :], ps_logit[:, 0:GT], ACT.Copy).then_inc(logit_copied, 1)
                run_bodies(act, body, *RUN)

            @block.vector
            def _(dve):
                def rest(g, q, c):
                    dve.wait_ge(high, g * HC + (c + 1))
                    nc.vector.tensor_tensor(cols(hl[q], c), cols(hidden, c), cols(hh[q], c).bitcast(F32),
                                            ALU.subtract).then_inc(low, 1)

                def choose(g, q):
                    dve.wait_ge(logit_turned, g + 1)
                    k = [0]

                    def step(ins):
                        k[0] += 1
                        ins.then_inc(choice_step, 1)
                        dve.wait_ge(choice_step, g * STEPS + k[0])

                    step(nc.vector.tensor_reduce(
                        v3(small), ps_turn[0:T, :].rearrange("p (b n) -> p b n", b=GB)[:, :, 0:2 * NE]
                        .rearrange("p b (two e) -> p b e two", two=2),
                        axis=AX_X, op=ALU.add))
                    step(nc.vector.tensor_tensor(v3(small), v3(small),
                                                 P["gate2_bias"][:, :].unsqueeze(1).to_broadcast([T, GB, NE]), ALU.add))
                    nc.vector.tensor_copy(lg_all[:, bass.ds(g * GB, GB), :], v3(small))
                    first_argmax(nc, step, v3(small), P["rank"][:, :], top[:, :], v3(ties), v3(chosen[q]), (T, GB))
                    assert k[0] == STEPS

                def pick(g, q, b, edge):
                    n = g * GB + b
                    if edge is None or edge * GB + b >= 1:
                        dve.wait_ge(masked, n)
                    if edge is None or edge * GB + b >= 2:
                        dve.wait_ge(reduced, n - 1)
                    dve.wait_ge(downed, n + 1)
                    nc.vector.tensor_tensor(picked[b % 2][:, :].rearrange("p (e c) -> p e c", e=NE),
                                            ps_y[b][0:T, :].rearrange("p (e c) -> p e c", e=NE),
                                            over(chosen[q][:, b * NE:(b + 1) * NE], D), ALU.mult).then_inc(masked, 1)
                    if edge is None or edge * GB + b >= 1:
                        reduce(n - 1, (b - 1) % 2)

                def reduce(n, p):
                    nc.vector.tensor_reduce(P["xn"][:, bass.ds(n * D, D)],
                                            picked[p][:, :].rearrange("p (e c) -> p c e", e=NE),
                                            axis=AX_X, op=ALU.add).then_inc(reduced, 1)

                def body(g, q, edge):
                    ahead, main = within(edge, -1), within(edge, 0)
                    if main:
                        pick(g, q, 0, edge)
                    if ahead:
                        rest(g + 1, 1 - q, 0)
                        rest(g + 1, 1 - q, 1)
                    if main:
                        pick(g, q, 1, edge)
                        pick(g, q, 2, edge)
                    if ahead:
                        choose(g + 1, 1 - q)
                    if main:
                        pick(g, q, 3, edge)
                    if edge == NG - 1:
                        dve.wait_ge(masked, B)
                        reduce(B - 1, 1)
                run_bodies(dve, body, *RUN)

        peak = scratch("peak", [T, B])
        OB = 32
        peaked = sem("fin_peaked")
        less = sem("fin_less")
        exps = sem("fin_exps")
        totals = sem("fin_totals")
        inverse = sem("fin_inverse")
        scaled = sem("fin_scaled")
        ready = sem("fin_ready")
        stored = sem("fin_stored")
        hb = halves(P["h"][:, :], B)
        yb = halves(P["xn"][:, :], B)
        with nc.Block() as block:
            @block.vector
            def _(dve):
                nc.vector.tensor_reduce(peak[:, :], lg_all, axis=AX_X, op=ALU.max).then_inc(peaked, 1)
                dve.wait_ge(peaked, 1)
                nc.vector.tensor_tensor(lg_all, lg_all, over(peak[:, :], NE), ALU.subtract).then_inc(less, 1)
                dve.wait_ge(exps, 1)
                nc.vector.tensor_reduce(peak[:, :], lg_all, axis=AX_X, op=ALU.add).then_inc(totals, 1)
                dve.wait_ge(totals, 1)
                nc.vector.reciprocal(peak[:, :], peak[:, :]).then_inc(inverse, 1)
                dve.wait_ge(inverse, 1)
                for k in range(B // OB):
                    at = slice(k * OB, (k + 1) * OB)
                    nc.vector.tensor_tensor(yb[:, at, :], yb[:, at, :], over(peak[:, at], D),
                                            ALU.mult).then_inc(scaled, 1)
                    dve.wait_ge(scaled, k + 1)
                    nc.vector.tensor_tensor(yb[:, at, :], yb[:, at, :], hb[:, at, :], ALU.add).then_inc(ready, 1)

            @block.scalar
            def _(act):
                act.wait_ge(less, 1)
                nc.scalar.activation(logits[:, :], logits[:, :], ACT.Exp).then_inc(exps, 1)

            @block.sync
            def _(sp):
                for k in range(B // OB):
                    at = slice(k * OB, (k + 1) * OB)
                    sp.wait_ge(ready, k + 1)
                    sp.dma_start(A["out"][at].rearrange("b t d -> t b d"), yb[:, at, :]).then_inc(stored, 16)
                sp.wait_ge(stored, 16 * (B // OB))


def program(nc, A):
    tok_dram = nc.dram_tensor("tok_dram", (B, TI, D), F32, kind="Internal").ap()
    gates_dram = nc.dram_tensor("gates_dram", (2 * NE, B, T), F32, kind="Internal").ap()
    cpad_dram = nc.dram_tensor("cpad_dram", (D, 2 * T), F32, kind="Internal").ap()
    with ExitStack() as ctx:
        def sb(name, shape, dt=F32):
            return ctx.enter_context(nc.sbuf_tensor(name, shape, dt))

        def sem(name):
            return ctx.enter_context(nc.semaphore(name))

        P = dict(
            h=sb("h", [T, B * D]),
            xs=sb("xs", [128, B * T], F32R),
            up_high=sb("up_high", [128, NE * D], F32R), up_low=sb("up_low", [128, NE * D], F32R),
            router=sb("router", [128, 2 * NE], F32R),
            down=sb("down", [128, CH * D]), up_bias=sb("up_bias", [128, CH]), down_bias=sb("down_bias", [2 * NE, D]),
            sel=sb("sel", [2 * NE, CH * 128], F32R),
            score_high=sb("score_high", [128, HEADS * D], F32R), score_low=sb("score_low", [128, HEADS * D], F32R),
            value=sb("value", [128, CH * D]),
            up2_high=sb("up2_high", [128, HID], F32R), up2_low=sb("up2_low", [128, HID], F32R),
            up2_bias=sb("up2_bias", [128, HC]),
            gate2=sb("gate2", [128, HC * 128], F32R), gate2_bias=sb("gate2_bias", [T, NE]),
            down2_high=sb("down2_high", [128, HC * NE * D], F32R), down2_low=sb("down2_low", [128, HC * NE * D], F32R),
            down2_bias=sb("down2_bias", [33, NE * D], F32R), ones=sb("ones", [33, T], F32R),
            ident=sb("ident", [128, 128]), rank=sb("rank", [T, NE]),
            norm_consts=[sb(f"norm_consts{i}", [T, LB]) for i in range(2)],
            tok_dram=tok_dram, cpad_dram=cpad_dram, gates=gates_dram)

        def phase(fn):
            with ExitStack() as banks:
                fn(nc, sb, lambda name, shape: banks.enter_context(nc.psum_tensor(name, shape, F32)), sem, A, P)

        phase(prepare)
        phase(tokens)
        phase(convolution)
        phase(route)
        P["xn"] = sb("xn_all", [T, B * D])
        phase(experts)
        phase(attention)
        phase(last_layer)



def _resize(n):
    scale = n / G8
    centre = (np.arange(G8) + 0.5) * scale - 0.5
    w = np.maximum(0.0, 1.0 - np.abs(centre[:, None] - np.arange(n)[None, :]) / max(scale, 1.0))
    return w / w.sum(1, keepdims=True)


def _constants():
    def haar(n, sign):
        m = np.zeros((n // 2, n))
        m[np.arange(n // 2), np.arange(0, n, 2)] = 0.7071067811865476
        m[np.arange(n // 2), np.arange(1, n, 2)] = sign * 0.7071067811865476
        return m

    half, quarter = IMG // 2, IMG // 4
    lo1, hi1 = haar(IMG, 1), haar(IMG, -1)
    filt = [_resize(quarter) @ haar(half, 1) @ lo1, _resize(quarter) @ haar(half, -1) @ lo1,
            _resize(half) @ lo1, _resize(half) @ hi1]
    rows = np.concatenate([f.T for f in filt], 1)
    maps = [(0, 0), (1, 0), (0, 1), (1, 1), (3, 2), (2, 3), (3, 3)]
    cols = np.zeros((IMG, 4, NMAP, G8))
    for m, (r, c) in enumerate(maps):
        cols[:, r, m, :] = filt[c].T
    sel = np.zeros((2, NE, CH, 2, D))
    for e in range(NE):
        sel[:, e, e // 2, e % 2, :] = 1.0
    f = np.float32
    return {"c_rows": rows.astype(f), "c_cols": cols.reshape(IMG, -1).astype(f), "c_ident": np.eye(128, dtype=f),
            "c_rank": np.tile(NE - np.arange(NE, dtype=f), (T, 1)), "c_sel": sel.reshape(2 * NE, CH * 128).astype(f)}


_INS = ['x', 'txt', 'L0_tok_W', 'L0_tok_b', 'L0_attn_c', 'L0_ffn_router_w', 'L0_ffn_w1', 'L0_ffn_b1', 'L0_ffn_w2',
        'L0_ffn_b2', 'L1_attn_Wq', 'L1_attn_Wk', 'L1_attn_Wv', 'L1_attn_Wo', 'L1_ffn_W1', 'L1_ffn_b1', 'L1_ffn_Wg',
        'L1_ffn_bg', 'L1_ffn_Wd', 'L1_ffn_bd']


def kernel(**inputs):
    import concourse.bacc as bacc
    from concourse.bass_utils import run_bass_kernel_spmd

    nc = bacc.Bacc("TRN2", target_bir_lowering=False, num_devices=1)
    arrays, A = {}, {}
    for name, a in [(n, inputs[n]) for n in _INS] + list(_constants().items()):
        a = np.ascontiguousarray(a)
        arrays[f"in_{name}"] = a
        A[name] = nc.dram_tensor(f"in_{name}", a.shape, mybir.dt.from_np(a.dtype), kind="ExternalInput").ap()
    A["out"] = nc.dram_tensor("out_0", (B, T, D), F32, kind="ExternalOutput").ap()
    program(nc, A)
    r = run_bass_kernel_spmd(nc, [arrays], core_ids=[0])
    return r.results[0]["out_0"]
```

```python
import numpy as np
from contextlib import ExitStack

import concourse.bass as bass
from concourse import mybir

F32 = mybir.dt.float32
F32R = mybir.dt.float32r
ALU = mybir.AluOpType
ACT = mybir.ActivationFunctionType
AX_X = mybir.AxisListType.X

B = 128
IMG = 84
G8 = 8
T = 96
TI = G8 * G8
D = 64
NMAP = 7
NE = 8
HEADS = 8
GB = 4
GT = GB * T
NG = B // GB
CH = NE * D // 128
HID = 256
HC = HID // 128
LB = 16
NLG = B // LB
EPS = 1e-5


def halves(ap, n):
    return ap.rearrange("p (b x) -> p b x", b=n)


def backwards(ap):
    *outer, (step, n) = [list(d) for d in ap.ap]
    return bass.AP(tensor=ap.tensor, offset=ap.offset + (n - 1) * step, ap=[*outer, [-step, n]])


def over(ap, n):
    return ap.unsqueeze(2).to_broadcast([ap.shape[0], ap.shape[1], n])



class Norm:

    def __init__(self, sb, sem, tag, nb):
        def two(name, cols):
            return [sb(f"{tag}_{name}{i}", [T, cols], F32) for i in range(2)]

        self.nb = nb
        self.total, self.power, self.variance, self.rstd = (two(n, nb) for n in ("total", "power", "variance", "rstd"))
        self.centred, self.square = two("centred", nb * D), two("square", nb * D)
        self.summed = sem(f"{tag}_summed")
        self.centred_ready = sem(f"{tag}_centred")
        self.squared = sem(f"{tag}_squared")
        self.power_ready = sem(f"{tag}_power")
        self.variance_ready = sem(f"{tag}_variance")
        self.rstd_ready = sem(f"{tag}_rstd")
        self.normed = sem(f"{tag}_normed")


def norm_sum(nc, dve, L, h, q):
    nc.vector.tensor_reduce(L.total[q][:, :], h, axis=AX_X, op=ALU.add).then_inc(L.summed, 1)


def norm_centre(nc, dve, L, h, t, q):
    dve.wait_ge(L.summed, t + 1)
    nc.vector.scalar_tensor_tensor(out=halves(L.centred[q][:, :], L.nb), in0=over(L.total[q][:, :], D),
                                   scalar=-1.0 / D, in1=h, op0=ALU.mult, op1=ALU.add).then_inc(L.centred_ready, 1)


def norm_square(nc, act, L, t, q):
    act.wait_ge(L.centred_ready, t + 1)
    nc.scalar.activation(L.square[q][:, :], L.centred[q][:, :], ACT.Square).then_inc(L.squared, 1)


def norm_power(nc, dve, L, t, q):
    dve.wait_ge(L.squared, t + 1)
    nc.vector.tensor_reduce(L.power[q][:, :], halves(L.square[q][:, :], L.nb), axis=AX_X,
                            op=ALU.add).then_inc(L.power_ready, 1)


def norm_rstd(nc, pool, L, consts, t, q):
    pool.wait_ge(L.power_ready, t + 1)
    nc.gpsimd.tensor_tensor(L.variance[q][:, :], L.power[q][:, :], consts[1][:, 0:L.nb],
                            ALU.add).then_inc(L.variance_ready, 1)
    pool.wait_ge(L.variance_ready, t + 1)
    nc.gpsimd.tensor_tensor(L.rstd[q][:, :], L.variance[q][:, :], consts[0][:, 0:L.nb],
                            ALU.pow).then_inc(L.rstd_ready, 1)


def norm_scale(nc, dve, L, out, t, q):
    dve.wait_ge(L.rstd_ready, t + 1)
    nc.vector.scalar_tensor_tensor(out=out, in0=halves(L.centred[q][:, :], L.nb), scalar=float(D) ** 0.5,
                                   in1=over(L.rstd[q][:, :], D), op0=ALU.mult, op1=ALU.mult).then_inc(L.normed, 1)



class Split:

    def __init__(self, sb, sem, tag, nb):
        self.nb = nb
        self.pair = [sb(f"{tag}_pair{i}", [T, nb * 2 * D], F32R) for i in range(2)]
        self.high = sem(f"{tag}_high")
        self.low = sem(f"{tag}_low")
        self.turned = sem(f"{tag}_turned")
        self.stored = sem(f"{tag}_stored")


def part(S, q, i):
    return S.pair[q][:, :].rearrange("p (b two x) -> p b two x", b=S.nb, two=2)[:, :, i, :]


def split_high(nc, act, L, S, xn, t, q):
    act.wait_ge(L.normed, t + 1)
    nc.scalar.activation(part(S, q, 0), xn, ACT.Copy).then_inc(S.high, 1)


def split_low(nc, dve, S, xn, t, q):
    dve.wait_ge(S.high, t + 1)
    nc.vector.tensor_tensor(part(S, q, 1), xn, part(S, q, 0).bitcast(F32), ALU.subtract).then_inc(S.low, 1)


def split_turn(nc, pe, S, ident, ps, t, q, first, n):
    for b in range(n):
        last = nc.tensor.transpose(ps[:, b * T:(b + 1) * T],
                                   S.pair[q][:, (first + b) * 2 * D:(first + b + 1) * 2 * D].bitcast(F32),
                                   ident[0:T, 0:T])
    last.then_inc(S.turned, 1)



def front(nc, sb, pb, sem, A, P):
    CB = 16
    NC = B // CB
    R = 4 * G8
    MAPS = NMAP * G8
    with ExitStack() as tmp:
        def scratch(name, shape, dt=F32):
            return tmp.enter_context(nc.sbuf_tensor(name, shape, dt))

        x = scratch("image", [IMG, B * IMG])
        rows = scratch("row_filters", [IMG, R])
        cols = scratch("col_filters", [IMG, 4 * MAPS])
        z = scratch("row_filtered", [IMG, 4 * B * G8])
        maps = scratch("maps", [MAPS + 1, B * G8])
        proj = scratch("projection", [MAPS + 1, G8 * D])
        tok = P["token_tiles"]
        up = scratch("up_raw", [128, NE * D])
        router = scratch("router_raw", [128, NE])
        wq, wk, wv, wo = P["wq_raw"], P["wk_raw"], P["wv_raw"], P["wo_raw"]
        up2 = scratch("up2_raw", [128, HID])
        gate2 = scratch("gate2_raw", [128, HC * NE])
        down2 = scratch("down2_raw", [128, HC * NE * D])
        bias_row = scratch("bd_raw", [1, NE * D])
        bias_low = scratch("bd_low", [1, NE * D])
        ones = scratch("ones_raw", [128, 128])
        zeros = scratch("zeros_raw", [128, 512])
        taps = scratch("taps", [D, D])
        cpad = scratch("cpad", [D, 2 * T])
        sel_raw = scratch("sel_raw", [2 * NE, CH * 128])
        ps = [pb(f"front_ps{i}", [128, 512]) for i in range(8)]
        filters = sem("filters_loaded")
        images = [sem(f"image_loaded{k}") for k in range(NC)]
        cleared = sem("projection_cleared")
        projection = sem("projection_loaded")
        filtered = sem("rows_filtered")
        copied = sem("rows_copied")
        mapped = sem("maps_ready")
        kept = sem("maps_copied")
        projected = sem("tokens_projected")
        evacuated = sem("tokens_copied")
        stored = P["tokens_stored"]
        arrived, text = P["tokens_arrived"], P["text_arrived"]
        taps_loaded = sem("taps_loaded")
        loaded = sem("weights_loaded")
        padded = sem("filter_padded")
        reversed_taps = sem("filter_reversed")
        zeroed = sem("weights_zeroed")
        split = sem("weights_split")
        zv = z[:, :].rearrange("p (r n) -> p r n", r=4)

        w1 = A["L0_ffn_w1"].rearrange("e d f -> d e f")
        loads = []
        for s in range(2):
            at = slice(s * D, (s + 1) * D)
            loads += [(up[at, :].rearrange("p (e f) -> p e f", e=NE), w1),
                      (router[at, :], A["L0_ffn_router_w"].rearrange("e d -> d e")),
                      (wq[at, :], A["L1_attn_Wq"]), (wk[at, :], A["L1_attn_Wk"]), (wv[at, :], A["L1_attn_Wv"]),
                      (up2[at, :], A["L1_ffn_W1"])]
        loads += [(wo[:, :], A["L1_attn_Wo"].rearrange("(u h) c -> u (h c)", h=HEADS)),
                  (P["down"][:, :].rearrange("p (k c) -> p k c", k=CH),
                   A["L0_ffn_w2"].rearrange("(k two) f c -> (two f) k c", two=2)),
                  (P["up_bias"][:, :], A["L0_ffn_b1"].rearrange("(k two) f -> (two f) k", two=2)),
                  (P["down_bias"][0:NE, :], A["L0_ffn_b2"]), (P["down_bias"][NE:2 * NE, :], A["L0_ffn_b2"]),
                  (P["up2_bias"][:, :], A["L1_ffn_b1"].rearrange("(k p) -> p k", p=128)),
                  (gate2[:, :].rearrange("p (k e) -> p k e", k=HC), A["L1_ffn_Wg"].rearrange("(k p) e -> p k e", p=128)),
                  (P["gate2_bias"][:, :], A["L1_ffn_bg"].unsqueeze(0).to_broadcast([T, NE])),
                  (bias_row[:, :].rearrange("a (e c) -> a e c", e=NE), A["L1_ffn_bd"].unsqueeze(0)),
                  (P["ident"][:, :], A["c_ident"]), (P["rank"][:, :], A["c_rank"]),
                  (sel_raw[:, :], A["c_sel"])]
        for k in range(HC):
            loads.append((down2[:, k * NE * D:(k + 1) * NE * D].rearrange("p (e c) -> p e c", e=NE),
                          A["L1_ffn_Wd"][:, k * 128:(k + 1) * 128, :].rearrange("e p c -> p e c")))
        n_loads = len(loads) * 16

        with nc.Block() as block:
            @block.sync
            def _(sp):
                sp.dma_start(rows[:, :], A["c_rows"]).then_inc(filters, 16)
                for k in range(NC):
                    sp.dma_start(x[:, k * CB * IMG:(k + 1) * CB * IMG].rearrange("p (b c) -> p b c", b=CB),
                                 A["x"][k * CB:(k + 1) * CB, 0].rearrange("b r c -> r b c")).then_inc(images[k], 16)
                    if k == 0:
                        sp.dma_start(cols[:, :], A["c_cols"]).then_inc(filters, 16)
                sp.wait_ge(reversed_taps, 1)
                sp.dma_start(P["cpad_dram"], cpad[:, :]).then_inc(padded, 16)
                sp.dma_start(halves(P["h"][TI:T, :], B), A["txt"].rearrange("b t d -> t b d")).then_inc(text, 16)
                for k in range(NC):
                    sp.wait_ge(evacuated, k + 1)
                    sp.dma_start(P["tok_dram"][k * CB:(k + 1) * CB].rearrange("b (i j) d -> (b i) (j d)", j=G8),
                                 tok[k % 4][:, :]).then_inc(stored[k % 4], 16)
                    if k in (1, 3):
                        for i in (k - 1, k):
                            sp.wait_ge(stored[i % 4], 16 * (i // 4 + 1))
                        n = 2 * CB
                        b0 = (k - 1) * CB
                        sp.dma_start(halves(P["h"][0:TI, b0 * D:(b0 + n) * D], n),
                                     P["tok_dram"][b0:b0 + n].rearrange("b t d -> t b d")).then_inc(arrived[k // 2], 16)
                sp.wait_ge(padded, 16)
                sp.wait_ge(filters, 32)

            @block.gpsimd
            def _(pool):
                nc.gpsimd.memset(ones[:, :], 1.0).then_inc(zeroed, 1)
                nc.gpsimd.memset(zeros[:, :], 0.0).then_inc(zeroed, 1)
                nc.gpsimd.memset(cpad[:, :], 0.0).then_inc(zeroed, 1)
                nc.gpsimd.memset(P["norm_consts"][0][:, :], -0.5)
                nc.gpsimd.memset(P["norm_consts"][1][:, :], D * EPS)
                nc.gpsimd.memset(proj[:, :], 0.0).then_inc(cleared, 1)
                nc.gpsimd.memset(maps[:, :], 1.0).then_inc(cleared, 1)
                pool.wait_ge(cleared, 2)
                for j in range(G8):
                    pool.dma_start(proj[j:j + (NMAP - 1) * G8 + 1:G8, j * D:(j + 1) * D],
                                   A["L0_tok_W"]).then_inc(projection, 16)
                    pool.dma_start(proj[MAPS:MAPS + 1, j * D:(j + 1) * D],
                                   A["L0_tok_b"].unsqueeze(0)).then_inc(projection, 16)
                pool.wait_ge(projection, 2 * G8 * 16)

            @block.tensor
            def _(pe):
                def row_filters(k):
                    pe.wait_ge(images[k], 16)
                    if k >= 4:
                        pe.wait_ge(copied, k - 3)
                    for b in range(CB):
                        at = (k * CB + b) * IMG
                        last = nc.tensor.matmul(ps[k % 4][0:IMG, b * R:(b + 1) * R], x[:, at:at + IMG],
                                                rows[:, :], start=True, stop=True)
                    last.then_inc(filtered, 1)

                def column_filters(n):
                    pe.wait_ge(copied, 4 * n + 4)
                    for r in range(4):
                        last = nc.tensor.matmul(ps[4 + n][0:MAPS, :], cols[:, r * MAPS:(r + 1) * MAPS],
                                                z[:, r * B * G8 + n * 512:r * B * G8 + (n + 1) * 512],
                                                start=(r == 0), stop=(r == 3))
                    last.then_inc(mapped, 1)

                def project(k):
                    pe.wait_ge(kept, k // 4 + 1)
                    if k >= 2:
                        pe.wait_ge(evacuated, k - 1)
                    nc.tensor.matmul(ps[6 + k % 2][:, :], maps[:, k * 128:(k + 1) * 128], proj[:, :],
                                     start=True, stop=True).then_inc(projected, 1)

                pe.wait_ge(filters, 32)
                for k in range(NC):
                    row_filters(k)
                    if k == 4:
                        column_filters(0)
                    if k == 5:
                        pe.wait_ge(projection, 2 * G8 * 16)
                        for i in range(4):
                            project(i)
                column_filters(1)
                for i in range(4, NC):
                    project(i)

            @block.scalar
            def _(act):
                with nc.allow_non_contiguous_dma(reason="a few small transposed weights"):
                    act.dma_start(taps[:, :], A["L0_attn_c"][0]).then_inc(taps_loaded, 16)
                    for dst, src in loads:
                        act.dma_start(dst, src).then_inc(loaded, 16)
                for k in range(NC):
                    act.wait_ge(projected, k + 1)
                    if k >= 4:
                        act.wait_ge(stored[k % 4], 16 * (k // 4))
                    nc.scalar.activation(tok[k % 4][:, :], ps[6 + k % 2][:, :], ACT.Copy).then_inc(evacuated, 1)

            @block.vector
            def _(dve):
                dve.wait_ge(zeroed, 3)
                dve.wait_ge(taps_loaded, 16)
                nc.vector.tensor_copy(cpad[:, T - D:T], backwards(taps[:, :])).then_inc(reversed_taps, 1)
                dve.wait_ge(cleared, 2)
                for k in range(NC):
                    dve.wait_ge(filtered, k + 1)
                    nc.vector.tensor_copy(
                        zv[:, :, k * CB * G8:(k + 1) * CB * G8].rearrange("p r (b i) -> p r b i", i=G8),
                        ps[k % 4][0:IMG, :].rearrange("p (b r i) -> p r b i", r=4, i=G8)).then_inc(copied, 1)
                    if k in (4, NC - 1):
                        n = 0 if k == 4 else 1
                        dve.wait_ge(mapped, n + 1)
                        nc.vector.tensor_copy(maps[0:MAPS, n * 512:(n + 1) * 512], ps[4 + n][0:MAPS, :]).then_inc(kept, 1)
                dve.wait_ge(loaded, n_loads)
                count = [0]

                def done(ins):
                    count[0] += 1
                    ins.then_inc(split, 1)

                def both(high, low, src):
                    done(nc.vector.tensor_copy(high, src))
                    dve.wait_ge(split, count[0])
                    done(nc.vector.tensor_tensor(low, src, high.bitcast(F32), ALU.subtract))

                both(P["up_high"][:, :], P["up_low"][:, :], up[:, :])
                both(P["router"][:, 0:NE], P["router"][:, NE:2 * NE], router[:, :])
                both(P["up2_high"][:, :], P["up2_low"][:, :], up2[:, :])
                both(P["down2_high"][:, :], P["down2_low"][:, :], down2[:, :])
                done(nc.vector.tensor_copy(P["gate2"][:, :], zeros[:, 0:HC * 128]))
                dve.wait_ge(split, count[0])
                for k in range(HC):
                    both(P["gate2"][:, k * 128:k * 128 + NE], P["gate2"][:, k * 128 + NE:k * 128 + 2 * NE],
                         gate2[:, k * NE:(k + 1) * NE])
                done(nc.vector.tensor_copy(P["ones"][:, :], ones[0:33, 0:T]))
                done(nc.vector.tensor_copy(P["down2_bias"][:, :], zeros[0:33, :]))
                dve.wait_ge(split, count[0])
                done(nc.vector.tensor_copy(P["down2_bias"][0:1, :], bias_row[:, :]))
                dve.wait_ge(split, count[0])
                done(nc.vector.tensor_tensor(bias_low[:, :], bias_row[:, :], P["down2_bias"][0:1, :].bitcast(F32),
                                             ALU.subtract))
                dve.wait_ge(split, count[0])
                done(nc.vector.tensor_copy(P["down2_bias"][32:33, :], bias_low[:, :]))
                done(nc.vector.tensor_copy(P["sel"][:, :], sel_raw[:, :]))



def convolution(nc, sb, pb, sem, A, P):
    QC = 4
    with ExitStack() as tmp:
        def scratch(name, shape, dt=F32):
            return tmp.enter_context(nc.sbuf_tensor(name, shape, dt))

        toeplitz = scratch("toeplitz", [T, D * T])
        u = scratch("conv_in", [T, D * B])
        wq, wk, wv, wo = P["wq_raw"], P["wk_raw"], P["wv_raw"], P["wo_raw"]
        turned = [scratch(f"{n}_turned", [D, HEADS * 128]) for n in ("wq", "wk", "wv")]
        stored, arrived = P["tokens_stored"], P["tokens_arrived"]
        wt = sem("weights_turned")
        wc = sem("weights_copied")
        folded = sem("weights_folded")
        fold_read = sem("weights_fold_read")
        L = Norm(scratch, sem, "ln1", LB)
        ps = [pb(f"conv_ps{i}", [128, 512]) for i in range(8)]
        fold, values = ps[6], ps[7]
        CD = D // 4
        hankel = [scratch(f"hankel{i}", [T, CD * T]) for i in range(2)]
        taps = [sem(f"hankel_loaded{i}") for i in range(2)]
        reversed_rows = sem("toeplitz_ready")
        by_channel = lambda t: t.rearrange("p (d t) -> p d t", t=T)
        convolved = sem("convolved")
        added = sem("conv_added")
        uv = u[:, :].rearrange("p (d b) -> p b d", b=B)
        hv = P["h"][:, :].rearrange("p (b d) -> p d b", d=D)
        hb = halves(P["h"][:, :], B)

        with nc.Block() as block:
            @block.sync
            def _(sp):
                pad = P["cpad_dram"]

                def load_tokens(half):
                    for s in stored[half * 2:half * 2 + 2]:
                        sp.wait_ge(s, 32)
                    n = B // 4
                    b0 = B // 2 + half * n
                    sp.dma_start(halves(P["h"][0:TI, b0 * D:(b0 + n) * D], n),
                                 P["tok_dram"][b0:b0 + n].rearrange("b t d -> t b d")).then_inc(arrived[2 + half], 16)

                for k in range(4):
                    if k < 2:
                        load_tokens(k)
                    if k >= 2:
                        sp.wait_ge(reversed_rows, k - 1)
                    src = bass.AP(tensor=pad.tensor, offset=pad.offset + k * CD * 2 * T,
                                  ap=[[1, T], [2 * T, CD], [1, T]])
                    sp.dma_start(by_channel(hankel[k % 2][:, :]), src).then_inc(taps[k % 2], 16)
                for s in taps:
                    sp.wait_ge(s, 32)

            @block.vector
            def _(dve):
                group = lambda t: hb[:, t * LB:(t + 1) * LB, :]
                dve.wait_ge(P["text_arrived"], 16)
                for t in range(-1, NLG + 1):
                    if 0 <= t < NLG:
                        if t >= 2:
                            dve.wait_ge(L.normed, t - 1)
                        norm_centre(nc, dve, L, group(t), t, t % 2)
                    if t + 1 < NLG:
                        if t % 2:
                            dve.wait_ge(arrived[(t + 1) // 2], 16)
                        norm_sum(nc, dve, L, group(t + 1), (t + 1) % 2)
                    if 0 <= t < NLG:
                        norm_power(nc, dve, L, t, t % 2)
                    if t >= 1:
                        norm_scale(nc, dve, L, uv[:, (t - 1) * LB:t * LB, :], t - 1, (t - 1) % 2)
                dve.wait_ge(fold_read, 2)
                nc.vector.tensor_tensor(P["score_low"][:, :], fold[:, :], P["score_high"][:, :].bitcast(F32),
                                        ALU.subtract).then_inc(fold_read, 1)
                for n in range(D // QC):
                    dve.wait_ge(convolved, n + 1)
                    at = hv[:, n * QC:(n + 1) * QC, :]
                    nc.vector.tensor_tensor(at, at, ps[n % 8][0:T, :].rearrange("p (c b) -> p c b", c=QC),
                                            ALU.add).then_inc(added, 1)

            @block.scalar
            def _(act):
                for t in range(NLG):
                    norm_square(nc, act, L, t, t % 2)
                    if t == 3:
                        act.wait_ge(wt, 1)
                        for n in range(6):
                            nc.scalar.activation(turned[n // 2][:, (n % 2) * 512:(n % 2 + 1) * 512], ps[n][0:D, :],
                                                 ACT.Copy).then_inc(wc, 1)
                    if t == 6:
                        act.wait_ge(folded, 1)
                        nc.scalar.activation(P["score_high"][:, :], fold[:, :], ACT.Copy).then_inc(fold_read, 1)
                        nc.scalar.activation(P["value"][:, :], values[:, 0:CH * D], ACT.Copy).then_inc(fold_read, 1)
                    k = t - 2
                    if 0 <= k < 4:
                        act.wait_ge(taps[k % 2], 16 * (k // 2 + 1))
                        nc.scalar.activation(by_channel(toeplitz[:, k * CD * T:(k + 1) * CD * T]),
                                             backwards(by_channel(hankel[k % 2][:, :])),
                                             ACT.Copy).then_inc(reversed_rows, 1)

            @block.gpsimd
            def _(pool):
                for t in range(NLG):
                    norm_rstd(nc, pool, L, P["norm_consts"], t, t % 2)

            @block.tensor
            def _(pe):
                for n, w in enumerate((wq, wk, wv)):
                    for h in range(HEADS):
                        bank = (n * 2 + h // 4)
                        last = nc.tensor.transpose(ps[bank][0:D, (h % 4) * 128:(h % 4 + 1) * 128],
                                                   w[:, h:h + (D - 1) * HEADS + 1:HEADS], P["ident"][:, :])
                last.then_inc(wt, 1)
                pe.wait_ge(wc, 6)
                for h in range(HEADS):
                    last = nc.tensor.matmul(fold[:, h * D:(h + 1) * D], turned[0][:, h * 128:(h + 1) * 128],
                                            turned[1][:, h * 128:h * 128 + D], start=True, stop=True)
                for h in range(HEADS):
                    s, k = h % 2, h // 2
                    last = nc.tensor.matmul(values[s * D:(s + 1) * D, k * D:(k + 1) * D],
                                            turned[2][:, h * 128:h * 128 + D], wo[:, h * D:(h + 1) * D],
                                            start=True, stop=True)
                last.then_inc(folded, 1)
                pe.wait_ge(fold_read, 3)
                pe.wait_ge(reversed_rows, 4)
                pe.wait_ge(L.normed, NLG)
                for n in range(D // QC):
                    if n >= 8:
                        pe.wait_ge(added, n - 7)
                    for c in range(QC):
                        d = n * QC + c
                        last = nc.tensor.matmul(ps[n % 8][0:T, c * B:(c + 1) * B], toeplitz[:, d * T:(d + 1) * T],
                                                u[:, d * B:(d + 1) * B], start=True, stop=True)
                    last.then_inc(convolved, 1)



def first_argmax(nc, step, probs, rank, largest, top, ties, out, shape):
    p, n = shape
    step(nc.vector.tensor_reduce(largest, probs, axis=AX_X, op=ALU.max))
    step(nc.vector.tensor_tensor(ties, probs, over(largest, NE), ALU.is_equal))
    step(nc.vector.tensor_tensor(ties, ties, rank.unsqueeze(1).to_broadcast([p, n, NE]), ALU.mult))
    step(nc.vector.tensor_reduce(top, ties, axis=AX_X, op=ALU.max))
    step(nc.vector.tensor_tensor(out, ties, over(top, NE), ALU.is_equal))


def route(nc, sb, pb, sem, A, P):
    RB = 8
    NRG = B // RB
    BPB = GB
    NBK = RB // BPB
    with ExitStack() as kept, ExitStack() as tmp:
        logits = kept.enter_context(nc.sbuf_tensor("logits", [T, B * NE], F32))

        def scratch(name, shape, dt=F32):
            return tmp.enter_context(nc.sbuf_tensor(name, shape, dt))

        L = Norm(scratch, sem, "ln2", RB)
        S = Split(scratch, sem, "ln2", RB)
        xn = [scratch(f"ln2_out{i}", [T, RB * D]) for i in range(2)]
        xs = [scratch(f"ln2_stack{i}", [128, RB * T], F32R) for i in range(2)]
        ps_turn = [pb(f"route_turn{i}", [128, 512]) for i in range(4)]
        ps_logit = [pb(f"route_logit{i}", [128, 512]) for i in range(2)]
        scored = sem("router_scored")
        gathered = sem("logits_ready")
        residual = sem("norm_added")
        stacked = [sem(f"stack_stored{i}") for i in range(2)]
        hb = halves(P["h"][:, :], B)
        lg = logits[:, :].rearrange("p (b e) -> p b e", e=NE)

        with nc.Block() as block:
            @block.vector
            def _(dve):
                group = lambda t: hb[:, t * RB:(t + 1) * RB, :]

                def collect(t):
                    dve.wait_ge(scored, t + 1)
                    nc.vector.tensor_reduce(
                        lg[:, t * RB:(t + 1) * RB, :],
                        ps_logit[t % 2][0:T, 0:RB * 2 * NE].rearrange("p (b two e) -> p b e two", two=2, e=NE),
                        axis=AX_X, op=ALU.add).then_inc(gathered, 1)

                for t in range(NRG + 2):
                    if t < NRG:
                        norm_sum(nc, dve, L, group(t), t % 2)
                        norm_centre(nc, dve, L, group(t), t, t % 2)
                    if 1 <= t <= NRG:
                        if t >= 3:
                            dve.wait_ge(residual, t - 2)
                        norm_scale(nc, dve, L, halves(xn[(t - 1) % 2][:, :], RB), t - 1, (t - 1) % 2)
                    if t < NRG:
                        norm_power(nc, dve, L, t, t % 2)
                    if 1 <= t <= NRG:
                        split_low(nc, dve, S, halves(xn[(t - 1) % 2][:, :], RB), t - 1, (t - 1) % 2)
                    if t >= 2:
                        collect(t - 2)

            @block.scalar
            def _(act):
                def evacuate(t):
                    if t >= 2:
                        act.wait_ge(scored, t - 1)
                        act.wait_ge(stacked[t % 2], 16 * (t // 2))
                    for k in range(NBK):
                        act.wait_ge(S.turned, t * NBK + k + 1)
                        nc.scalar.activation(xs[t % 2][:, k * GT:(k + 1) * GT], ps_turn[k][:, 0:GT],
                                             ACT.Copy).then_inc(S.stored, 1)

                for t in range(NRG + 2):
                    if t >= 2:
                        evacuate(t - 2)
                    if t < NRG:
                        norm_square(nc, act, L, t, t % 2)
                    if 1 <= t <= NRG:
                        if t >= 3:
                            act.wait_ge(S.turned, (t - 2) * NBK)
                        split_high(nc, act, L, S, halves(xn[(t - 1) % 2][:, :], RB), t - 1, (t - 1) % 2)

            @block.gpsimd
            def _(pool):
                for t in range(NRG + 1):
                    if t < NRG:
                        norm_rstd(nc, pool, L, P["norm_consts"], t, t % 2)
                    if t:
                        pool.wait_ge(L.normed, t)
                        at = P["h"][:, (t - 1) * RB * D:t * RB * D]
                        nc.gpsimd.tensor_tensor(at, at, xn[(t - 1) % 2][:, :], ALU.add).then_inc(residual, 1)

            @block.sync
            def _(sp):
                for t in range(NRG):
                    sp.wait_ge(S.stored, (t + 1) * NBK)
                    sp.dma_start(P["xs"][:, t * RB * T:(t + 1) * RB * T].bitcast(F32),
                                 xs[t % 2][:, :].bitcast(F32)).then_inc(stacked[t % 2], 16)
                for s in stacked:
                    sp.wait_ge(s, 8 * NRG)

            @block.tensor
            def _(pe):
                for t in range(NRG):
                    pe.wait_ge(S.low, t + 1)
                    for k in range(NBK):
                        if t:
                            pe.wait_ge(S.stored, (t - 1) * NBK + k + 1)
                        split_turn(nc, pe, S, P["ident"], ps_turn[k], t, t % 2, k * BPB, BPB)
                    pe.wait_ge(S.stored, (t + 1) * NBK)
                    if t >= 2:
                        pe.wait_ge(gathered, t - 1)
                    for b in range(RB):
                        last = nc.tensor.matmul(ps_logit[t % 2][0:T, b * 2 * NE:(b + 1) * 2 * NE],
                                                xs[t % 2][:, b * T:(b + 1) * T], P["router"][:, :],
                                                start=True, stop=True)
                    last.then_inc(scored, 1)

        tmp.close()
        probs = scratch("probs", [T, B * NE])
        ties = scratch("ties", [T, B * NE])
        first = scratch("first", [T, B * NE])
        second = scratch("second", [T, B * NE])
        top = scratch("top", [T, B])
        weight = [scratch(f"weight{i}", [T, B]) for i in range(2)]
        total = scratch("softmax_total", [T, B])
        gates = scratch("gates", [T, B * 2 * NE], F32R)
        turned_gates = scratch("turned_gates", [128, B // 8 * T], F32R)
        gates_stored = sem("gates_stored")
        PER = 8
        step_done = sem("gate_step")
        exps = sem("router_exp")
        gates_turned = sem("gates_turned")
        gates_copied = sem("gates_copied")
        v3 = lambda t: t[:, :].rearrange("p (b e) -> p b e", e=NE)

        with nc.Block() as block:
            @block.vector
            def _(dve):
                n = [0]

                def step(ins):
                    n[0] += 1
                    ins.then_inc(step_done, 1)
                    dve.wait_ge(step_done, n[0])

                step(nc.vector.tensor_reduce(top[:, :], lg, axis=AX_X, op=ALU.max))
                step(nc.vector.tensor_tensor(lg, lg, over(top[:, :], NE), ALU.subtract))
                dve.wait_ge(exps, 1)
                step(nc.vector.tensor_reduce(total[:, :], v3(probs), axis=AX_X, op=ALU.add))
                step(nc.vector.reciprocal(total[:, :], total[:, :]))
                step(nc.vector.tensor_tensor(v3(probs), v3(probs), over(total[:, :], NE), ALU.mult))
                first_argmax(nc, step, v3(probs), P["rank"][:, :], weight[0][:, :], top[:, :], v3(ties), v3(first),
                             (T, B))
                step(nc.vector.scalar_tensor_tensor(out=second[:, :], in0=first[:, :], scalar=-2.0, in1=probs[:, :],
                                                    op0=ALU.mult, op1=ALU.add))
                first_argmax(nc, step, v3(second), P["rank"][:, :], weight[1][:, :], top[:, :], v3(ties), v3(second),
                             (T, B))
                step(nc.vector.tensor_tensor(total[:, :], weight[0][:, :], weight[1][:, :], ALU.add))
                step(nc.vector.tensor_scalar(total[:, :], total[:, :], 1e-12, None, ALU.max))
                step(nc.vector.reciprocal(total[:, :], total[:, :]))
                step(nc.vector.tensor_tensor(first[:, :], first[:, :], second[:, :], ALU.add))
                step(nc.vector.tensor_tensor(v3(first), v3(first), over(total[:, :], NE), ALU.mult))
                step(nc.vector.tensor_tensor(first[:, :], first[:, :], probs[:, :], ALU.mult))
                gv = gates[:, :].rearrange("p (b two e) -> p b two e", two=2, e=NE)
                step(nc.vector.tensor_copy(gv[:, :, 0, :], v3(first)))
                step(nc.vector.tensor_tensor(gv[:, :, 1, :], v3(first), gv[:, :, 0, :].bitcast(F32), ALU.subtract))

            GATE_STEPS = 2 + 3 + 5 + 1 + 5 + 3 + 3 + 2

            @block.scalar
            def _(act):
                act.wait_ge(step_done, 2)
                nc.scalar.activation(probs[:, :], logits[:, :], ACT.Exp).then_inc(exps, 1)
                for k in range(4):
                    act.wait_ge(gates_turned, k + 1)
                    nc.scalar.activation(turned_gates[:, k * GT:(k + 1) * GT], ps_turn[k][:, 0:GT],
                                         ACT.Copy).then_inc(gates_copied, 1)

            @block.tensor
            def _(pe):
                pe.wait_ge(step_done, GATE_STEPS)
                for k in range(4):
                    for m in range(4):
                        at = (k * 4 + m) * PER * 2 * NE
                        last = nc.tensor.transpose(ps_turn[k][:, m * T:(m + 1) * T],
                                                   gates[:, at:at + PER * 2 * NE].bitcast(F32), P["ident"][0:T, 0:T])
                    last.then_inc(gates_turned, 1)

            @block.sync
            def _(sp):
                for k in range(4):
                    sp.wait_ge(gates_copied, k + 1)
                    sp.dma_start(P["gates"][:, k * GT:(k + 1) * GT],
                                 turned_gates[:, k * GT:(k + 1) * GT].bitcast(F32)).then_inc(gates_stored, 16)
                sp.wait_ge(gates_stored, 4 * 16)



def run_bodies(eng, body, first, last, steady_first, steady_last):
    assert (steady_last - steady_first + 1) % 2 == 0
    for g in range(first, steady_first):
        body(g, g % 2, g)
    with eng.Fori(0, (steady_last - steady_first + 1) // 2) as i:
        for k in range(2):
            body(i * 2 + (steady_first + k), (steady_first + k) % 2, None)
    for g in range(steady_last + 1, last + 1):
        body(g, g % 2, g)


class Half:

    def __init__(self, twice):
        self.twice = twice

    def __mul__(self, k):
        assert k % 2 == 0
        return self.twice * (k // 2)


def nth_of_parity(g, q):
    return Half(g + (2 - q))


def within(edge, shift, low=0):
    return edge is None or low <= edge - shift < NG


def at_least(edge, shift, low):
    return edge is None or edge - shift >= low


def experts(nc, sb, pb, sem, A, P):
    with ExitStack() as tmp:
        def scratch(name, shape, dt=F32):
            return tmp.enter_context(nc.sbuf_tensor(name, shape, dt))

        L = Norm(scratch, sem, "ln3", GB)
        S = Split(scratch, sem, "ln3", GB)
        hidden = scratch("hidden", [128, CH * GT])
        gated = scratch("gated", [128, CH * GT])
        gate = [scratch(f"gate_stage{i}", [2 * NE, GT], F32R) for i in range(2)]
        y = [scratch(f"expert_sum{i}", [128, GT // 2]) for i in range(2)]
        ps_up = [pb(f"ex_up{i}", [128, 512]) for i in range(2)]
        ps_gate = [pb(f"ex_gate{i}", [128, 512]) for i in range(CH)]
        ps_down = pb("ex_down", [128, 512])
        ps_misc = pb("ex_misc", [128, 512])
        upped = sem("ex_upped")
        gate_loaded = [sem(f"ex_gate_loaded{i}") for i in range(2)]
        gate_spread = sem("ex_gate_spread")
        activated = sem("ex_activated")
        gated_ready = sem("ex_gated")
        downed = sem("ex_downed")
        biased = sem("ex_biased")
        copied = sem("ex_copied")
        turned_back = sem("ex_turned_back")
        updated = sem("ex_updated")
        hb = halves(P["h"][:, :], B)
        xb = halves(P["xn"][:, :], B)
        h_at = lambda g: hb[:, bass.ds(g * GB, GB), :]
        xn_at = lambda g: xb[:, bass.ds(g * GB, GB), :]
        cols = lambda t, c: t[:, c * GT:(c + 1) * GT]
        RUN = (0, NG + 4, 6, NG - 1)
        WARM_UP = 16

        with nc.Block() as block:
            @block.sync
            def _(sp):
                gates = P["gates"].rearrange("(m r) n -> r m n", r=2 * NE)

                def body(g, q, edge):
                    if not within(edge, 0):
                        return
                    if at_least(edge, 0, 2):
                        sp.wait_ge(biased, g - 1)
                    sp.dma_start(gate[q][:, :].bitcast(F32).rearrange("r (b t) -> r b t", t=T),
                                 gates[:, q * GB:(q + 1) * GB, bass.ds((g - q) * (T // 2), T)]
                                 ).then_inc(gate_loaded[q], 16)
                run_bodies(sp, body, *RUN)

            @block.tensor
            def _(pe):
                def down(g, q, c, edge):
                    pe.wait_ge(gated_ready, g * CH + (c + 1))
                    if c == 0:
                        if at_least(edge, 1, 1):
                            pe.wait_ge(copied, g)
                        for s in range(2):
                            rhs = gate[q][:, :].bitcast(F32).rearrange("p (m s t) -> p m s t", s=2, t=T)[:, :, s, :]
                            last = nc.tensor.matmul(ps_down[s * D:(s + 1) * D, 0:GT // 2], P["down_bias"][:, :], rhs,
                                                    start=True, stop=False)
                        last.then_inc(biased, 1)
                    for s in range(2):
                        rhs = cols(gated, c).rearrange("p (m s t) -> p m s t", s=2, t=T)[:, :, s, :]
                        last = nc.tensor.matmul(ps_down[s * D:(s + 1) * D, 0:GT // 2],
                                                P["down"][:, c * D:(c + 1) * D], rhs, start=False, stop=(c == CH - 1))
                    last.then_inc(downed, 1)

                def body(g, q, edge):
                    for c in range(CH):
                        if within(edge, 1):
                            down(g - 1, 1 - q, c, edge)
                        if within(edge, 0):
                            n = g * CH + c
                            if edge is None or edge * CH + c >= 2:
                                pe.wait_ge(activated, n - 1)
                            x = P["xs"][:, bass.ds(g * GT, GT)]
                            nc.tensor.matmul(ps_up[c % 2][:, 0:GT], P["up_high"][:, c * 128:(c + 1) * 128], x,
                                             start=True, stop=False)
                            nc.tensor.matmul(ps_up[c % 2][:, 0:GT], P["up_low"][:, c * 128:(c + 1) * 128], x,
                                             start=False, stop=True).then_inc(upped, 1)
                            if c == 0:
                                pe.wait_ge(gate_loaded[q], nth_of_parity(g, q) * 16)
                            if at_least(edge, 0, 1):
                                pe.wait_ge(gated_ready, n - (CH - 1))
                            nc.tensor.matmul(ps_gate[c][:, 0:GT], P["sel"][:, c * 128:(c + 1) * 128],
                                             gate[q][:, :], start=True, stop=True).then_inc(gate_spread, 1)
                        if c == 0 and within(edge, 5):
                            pe.wait_ge(S.low, g - 4)
                            if within(edge, 3):
                                pe.wait_ge(updated, g - 2)
                            else:
                                pe.wait_ge(S.stored, g - 5)
                            split_turn(nc, pe, S, P["ident"], ps_misc, g - 5, 1 - q, 0, GB)
                        if c == 3 and within(edge, 2):
                            pe.wait_ge(copied, g - 1)
                            if at_least(edge, 5, 0):
                                pe.wait_ge(S.stored, g - 4)
                            elif at_least(edge, 3, 0):
                                pe.wait_ge(updated, g - 2)
                            for m in range(GB // 2):
                                last = nc.tensor.transpose(ps_misc[0:T, m * 128:(m + 1) * 128],
                                                           y[q][:, m * T:(m + 1) * T], P["ident"][:, :])
                            last.then_inc(turned_back, 1)
                for _ in range(WARM_UP):
                    nc.tensor.matmul(ps_misc[:, :], P["up_high"][:, 0:128], P["up_high"][:, :], start=True, stop=True)
                run_bodies(pe, body, *RUN)

            @block.scalar
            def _(act):
                def hidden_chunk(g, c, edge):
                    n = g * CH + c
                    act.wait_ge(upped, n + 1)
                    if at_least(edge, 0, 1):
                        act.wait_ge(gated_ready, n - 3)
                    nc.scalar.activation(cols(hidden, c), ps_up[c % 2][:, 0:GT], ACT.Gelu,
                                         bias=P["up_bias"][:, c:c + 1]).then_inc(activated, 1)

                def body(g, q, edge):
                    if within(edge, 0):
                        hidden_chunk(g, 0, edge)
                    if within(edge, 5):
                        act.wait_ge(S.turned, g - 4)
                        nc.scalar.activation(P["xs"][:, bass.ds((g - 5) * GT, GT)], ps_misc[:, 0:GT],
                                             ACT.Copy).then_inc(S.stored, 1)
                    if within(edge, 4):
                        split_high(nc, act, L, S, xn_at(g - 4), g - 4, q)
                    if within(edge, 3):
                        norm_square(nc, act, L, g - 3, 1 - q)
                    if within(edge, 0):
                        hidden_chunk(g, 1, edge)
                        hidden_chunk(g, 2, edge)
                    if within(edge, 1):
                        act.wait_ge(downed, g * CH)
                        if at_least(edge, 1, 2):
                            act.wait_ge(turned_back, g - 2)
                        nc.scalar.activation(y[1 - q][:, :], ps_down[:, 0:GT // 2], ACT.Copy).then_inc(copied, 1)
                    if within(edge, 0):
                        hidden_chunk(g, 3, edge)
                run_bodies(act, body, *RUN)

            @block.vector
            def _(dve):
                def gate_chunk(g, c, edge):
                    n = g * CH + c
                    dve.wait_ge(activated, n + 1)
                    dve.wait_ge(gate_spread, n + 1)
                    if at_least(edge, 0, 1):
                        dve.wait_ge(downed, n - (CH - 1))
                    nc.vector.tensor_tensor(cols(gated, c), cols(hidden, c), ps_gate[c][:, 0:GT],
                                            ALU.mult).then_inc(gated_ready, 1)

                def body(g, q, edge):
                    main, summed, scaled, split = (within(edge, s) for s in (0, 2, 3, 4))
                    if split:
                        split_low(nc, dve, S, xn_at(g - 4), g - 4, q)
                    if main:
                        gate_chunk(g, 0, edge)
                    if scaled:
                        norm_power(nc, dve, L, g - 3, 1 - q)
                    if main:
                        gate_chunk(g, 1, edge)
                        gate_chunk(g, 2, edge)
                    if summed:
                        dve.wait_ge(turned_back, g - 1)
                        nc.vector.tensor_tensor(h_at(g - 2), h_at(g - 2),
                                                ps_misc[0:T, 0:GB * D].rearrange("p (b x) -> p b x", b=GB),
                                                ALU.add).then_inc(updated, 1)
                        dve.wait_ge(updated, g - 1)
                    if scaled:
                        norm_scale(nc, dve, L, xn_at(g - 3), g - 3, 1 - q)
                    if summed:
                        norm_sum(nc, dve, L, h_at(g - 2), q)
                        norm_centre(nc, dve, L, h_at(g - 2), g - 2, q)
                    if main:
                        gate_chunk(g, 3, edge)
                run_bodies(dve, body, *RUN)

            @block.gpsimd
            def _(pool):
                def body(g, q, edge):
                    if within(edge, 3):
                        norm_rstd(nc, pool, L, P["norm_consts"], g - 3, 1 - q)
                run_bodies(pool, body, *RUN)


def attention(nc, sb, pb, sem, A, P):
    with ExitStack() as tmp:
        def scratch(name, shape, dt=F32):
            return tmp.enter_context(nc.sbuf_tensor(name, shape, dt))

        L = Norm(scratch, sem, "ln4", GB)
        S = Split(scratch, sem, "ln4", GB)
        xn = [scratch(f"ln4_out{i}", [T, GB * D]) for i in range(2)]
        x = [[scratch(f"x_{n}{i}", [128, GT], F32R) for n in ("rest_first", "rounded_first")] for i in range(2)]
        xt = [scratch(f"x_tokens{i}", [T, GB * D]) for i in range(2)]
        m = [scratch(f"xm{i}", [128, 2 * CH * GT], F32R) for i in range(2)]
        attn = [scratch(f"attn{i}", [T, HEADS * T]) for i in range(2)]
        ax = [scratch(f"attn_x{i}", [128, GB * CH * T]) for i in range(2)]
        y = [scratch(f"attn_sum{i}", [128, GT // 2]) for i in range(2)]
        ps_m = [pb(f"at_xm{i}", [128, 512]) for i in range(2)]
        ps_s = [pb(f"at_scores{i}", [128, 1024]) for i in range(2)]
        ps_x = pb("at_ax", [128, 512])
        ps_misc = pb("at_misc", [128, 512])
        staged = [sem(f"at_staged{i}") for i in range(2)]
        projected = sem("at_xm")
        high = sem("at_xm_high")
        low = sem("at_xm_low")
        scored = sem("at_scored")
        weighed = sem("at_weighed")
        applied = sem("at_applied")
        kept = sem("at_kept")
        summed = sem("at_summed")
        copied = sem("at_copied")
        turned_back = sem("at_turned_back")
        updated = sem("at_updated")
        hb = halves(P["h"][:, :], B)
        xb = halves(P["xn"][:, :], B)
        h_at = lambda g: hb[:, bass.ds(g * GB, GB), :]
        side = lambda t, s, k, half: t[half * D:(half + 1) * D, (s * CH + k) * GT:(s * CH + k + 1) * GT]
        RUN = (-1, NG + 3, 5, NG - 2)
        SEM = float(D) ** 0.5
        STAGED = 4 * 16

        with nc.Block() as block:
            @block.sync
            def _(sp):
                def body(g, q, edge):
                    if not within(edge, 0):
                        return
                    if at_least(edge, 0, 2):
                        sp.wait_ge(scored, g * GB - GB)
                        sp.wait_ge(applied, g * GB - GB)
                    sp.dma_start(x[q][1][:, :].bitcast(F32),
                                 P["xs"][:, bass.ds(g * GT, GT)].bitcast(F32)).then_inc(staged[q], 16)
                    for half in range(2):
                        sp.dma_start(x[q][0][half * D:(half + 1) * D, :].bitcast(F32),
                                     P["xs"][(1 - half) * D:(2 - half) * D, bass.ds(g * GT, GT)].bitcast(F32)
                                     ).then_inc(staged[q], 16)
                    sp.dma_start(xt[q][:, :], P["xn"][:, bass.ds(g * GB * D, GB * D)]).then_inc(staged[q], 16)
                run_bodies(sp, body, *RUN)

            @block.tensor
            def _(pe):
                def scores(g, q, b, edge):
                    n = g * GB + b
                    if b == 0:
                        pe.wait_ge(low, (g + 1) * 2 * CH)
                        pe.wait_ge(staged[q], nth_of_parity(g, q) * STAGED)
                    if edge is None or edge * GB + b >= 2:
                        pe.wait_ge(weighed, n - 1)
                    for s in range(2):
                        out = ps_s[b % 2][0:T, s * 512:s * 512 + CH * T]
                        mv = m[q][:, s * CH * GT:(s + 1) * CH * GT].rearrange("p (k b t) -> p k b t", k=CH,
                                                                              b=GB)[:, :, b, :]
                        tb = slice(b * T, (b + 1) * T)
                        at = slice(s * D, (s + 1) * D)
                        nc.tensor.matmul(out, x[q][s][:, tb], mv, start=True, stop=False)
                        last = nc.tensor.matmul(out, x[q][1 - s][at, tb], mv[at], start=False, stop=True)
                    last.then_inc(scored, 1)

                def project(g, k, edge):
                    if edge is None or (edge + 1) * CH + k >= 2:
                        pe.wait_ge(low, g * 2 * CH + 2 * (k - 1))
                    xs = P["xs"][:, bass.ds(g * GT, GT)]
                    nc.tensor.matmul(ps_m[k % 2][:, 0:GT], P["score_high"][:, k * 128:(k + 1) * 128], xs,
                                     start=True, stop=False)
                    nc.tensor.matmul(ps_m[k % 2][:, 0:GT], P["score_low"][:, k * 128:(k + 1) * 128], xs,
                                     start=False, stop=True).then_inc(projected, 1)

                def apply(g, q, b, edge, shift):
                    n = g * GB + b
                    pe.wait_ge(weighed, n + 1)
                    if edge is None or (edge - shift) * GB + b >= 1:
                        pe.wait_ge(kept, n)
                    for s in range(2):
                        last = nc.tensor.matmul(ps_x[s * D:(s + 1) * D, 0:CH * T], xt[q][:, b * D:(b + 1) * D],
                                                attn[b % 2][:, s * CH * T:(s + 1) * CH * T], start=True, stop=True)
                    last.then_inc(applied, 1)

                def body(g, q, edge):
                    for b in range(GB):
                        if within(edge, -1):
                            project(g + 1, b, edge)
                        if within(edge, 0):
                            scores(g, q, b, edge)
                        if b == 0 and within(edge, 1):
                            apply(g - 1, 1 - q, GB - 1, edge, 1)
                        if b and within(edge, 0):
                            apply(g, q, b - 1, edge, 0)
                        if b == 0 and within(edge, 4):
                            pe.wait_ge(S.low, g - 3)
                            pe.wait_ge(updated, g - 1 if edge is None else min(g - 1, NG))
                            if edge is not None and edge - 2 >= NG:
                                pe.wait_ge(S.stored, g - 4)
                            split_turn(nc, pe, S, P["ident"], ps_misc, g - 4, q, 0, GB)
                        if b == 1 and within(edge, 1):
                            pe.wait_ge(kept, g * GB)
                            if at_least(edge, 4, 0):
                                pe.wait_ge(S.stored, g - 3)
                            elif at_least(edge, 2, 0):
                                pe.wait_ge(updated, g - 1)
                            for s in range(2):
                                for k in range(CH):
                                    rhs = ax[1 - q][:, :].rearrange("p (m s k t) -> p m s k t", s=2, k=CH,
                                                                    t=T)[:, :, s, k, :]
                                    last = nc.tensor.matmul(ps_misc[s * D:(s + 1) * D, 0:GT // 2],
                                                            P["value"][:, k * D:(k + 1) * D], rhs,
                                                            start=(k == 0), stop=(k == CH - 1))
                            last.then_inc(summed, 1)
                        if b == 3 and within(edge, 1):
                            pe.wait_ge(copied, g)
                            for m in range(GB // 2):
                                last = nc.tensor.transpose(ps_misc[0:T, m * 128:(m + 1) * 128],
                                                           y[1 - q][:, m * T:(m + 1) * T], P["ident"][:, :])
                            last.then_inc(turned_back, 1)
                run_bodies(pe, body, *RUN)

            @block.scalar
            def _(act):
                def body(g, q, edge):
                    for b in range(GB):
                        if within(edge, -1):
                            k, n = b, (g + 1) * CH + b
                            act.wait_ge(projected, n + 1)
                            if at_least(edge, -1, 2):
                                act.wait_ge(scored, g * GB)
                            for s in range(2):
                                nc.scalar.activation(side(m[1 - q], s, k, s), ps_m[k % 2][s * D:(s + 1) * D, 0:GT],
                                                     ACT.Copy).then_inc(high, 1)
                        if within(edge, 0):
                            n = g * GB + b
                            act.wait_ge(scored, n + 1)
                            if edge is None or edge * GB + b >= 2:
                                act.wait_ge(applied, n - 1)
                            nc.scalar.activation(
                                attn[b % 2][:, :].rearrange("p (s n) -> p s n", s=2),
                                ps_s[b % 2][0:T, :].rearrange("p (s n) -> p s n", s=2)[:, :, 0:CH * T],
                                ACT.Sigmoid, scale=SEM).then_inc(weighed, 1)
                        if b == 1 and within(edge, 2):
                            norm_square(nc, act, L, g - 2, q)
                        if b == 0 and within(edge, 4):
                            act.wait_ge(S.turned, g - 3)
                            nc.scalar.activation(P["xs"][:, bass.ds((g - 4) * GT, GT)], ps_misc[:, 0:GT],
                                                 ACT.Copy).then_inc(S.stored, 1)
                        if b == 0 and within(edge, 3):
                            split_high(nc, act, L, S, halves(xn[1 - q][:, :], GB), g - 3, 1 - q)
                run_bodies(act, body, *RUN)

            @block.vector
            def _(dve):
                def rest(g, q, k):
                    dve.wait_ge(high, g * 2 * CH + 2 * (k + 1))
                    for s in range(2):
                        nc.vector.tensor_tensor(side(m[q], s, k, 1 - s), ps_m[k % 2][s * D:(s + 1) * D, 0:GT],
                                                side(m[q], s, k, s).bitcast(F32), ALU.subtract).then_inc(low, 1)

                def keep(g, q, b):
                    dve.wait_ge(applied, g * GB + (b + 1))
                    nc.vector.tensor_copy(ax[q][:, b * CH * T:(b + 1) * CH * T],
                                          ps_x[:, 0:CH * T]).then_inc(kept, 1)

                def body(g, q, edge):
                    ahead, main, mid, tail, last = (within(edge, s) for s in (-1, 0, 1, 2, 3))
                    if last:
                        norm_scale(nc, dve, L, halves(xn[1 - q][:, :], GB), g - 3, 1 - q)
                    if tail:
                        dve.wait_ge(updated, g - 1)
                    if mid:
                        keep(g - 1, 1 - q, GB - 1)
                    if ahead:
                        rest(g + 1, 1 - q, 0)
                    if tail:
                        norm_sum(nc, dve, L, h_at(g - 2), q)
                    if ahead:
                        rest(g + 1, 1 - q, 1)
                    if tail:
                        norm_centre(nc, dve, L, h_at(g - 2), g - 2, q)
                    if main:
                        keep(g, q, 0)
                    if last:
                        split_low(nc, dve, S, halves(xn[1 - q][:, :], GB), g - 3, 1 - q)
                    if mid:
                        dve.wait_ge(summed, g)
                        nc.vector.tensor_copy(y[1 - q][:, :], ps_misc[:, 0:GT // 2]).then_inc(copied, 1)
                    if tail:
                        norm_power(nc, dve, L, g - 2, q)
                    if ahead:
                        rest(g + 1, 1 - q, 2)
                    if main:
                        keep(g, q, 1)
                    if ahead:
                        rest(g + 1, 1 - q, 3)
                    if main:
                        keep(g, q, 2)
                    if mid:
                        dve.wait_ge(turned_back, g)
                        nc.vector.scalar_tensor_tensor(
                            out=h_at(g - 1), in0=ps_misc[0:T, 0:GB * D].rearrange("p (b x) -> p b x", b=GB),
                            scalar=0.0, in1=h_at(g - 1), op0=ALU.max, op1=ALU.add).then_inc(updated, 1)
                run_bodies(dve, body, *RUN)

            @block.gpsimd
            def _(pool):
                def body(g, q, edge):
                    if within(edge, 2):
                        norm_rstd(nc, pool, L, P["norm_consts"], g - 2, q)
                run_bodies(pool, body, *RUN)


def last_layer(nc, sb, pb, sem, A, P):
    with ExitStack() as tmp:
        def scratch(name, shape, dt=F32):
            return tmp.enter_context(nc.sbuf_tensor(name, shape, dt))

        hidden = scratch("hidden2", [128, HC * GT])
        hh = [scratch(f"hidden_high{i}", [128, HC * GT], F32R) for i in range(2)]
        hl = [scratch(f"hidden_low{i}", [128, HC * GT], F32R) for i in range(2)]
        lt = scratch("logits_turned", [128, GT])
        small = scratch("logits_now", [T, GB * NE])
        largest = scratch("largest_logit", [T, GB])
        less = [scratch(f"logits_less_max{i}", [T, GB * NE]) for i in range(2)]
        exps = scratch("logit_exps", [T, GB * NE])
        total = scratch("exp_total", [T, GB])
        share = [scratch(f"probability{i}", [T, GB]) for i in range(2)]
        y = [scratch(f"chosen_output{i}", [T, GB * D]) for i in range(2)]
        ties = scratch("ties2", [T, GB * NE])
        top = scratch("top2", [T, GB])
        chosen = [scratch(f"chosen{i}", [T, GB * NE]) for i in range(2)]
        picked = [scratch(f"picked{i}", [T, NE * D]) for i in range(GB)]
        ps_up = [pb(f"la_up{i}", [128, 512]) for i in range(2)]
        ps_logit = pb("la_logit", [128, 512])
        ps_turn = pb("la_turn", [128, 512])
        ps_y = [pb(f"la_y{i}", [128, 512]) for i in range(4)]
        upped = sem("la_upped")
        activated = sem("la_activated")
        high = sem("la_high")
        low = sem("la_low")
        scored = sem("la_scored")
        logit_copied = sem("la_logit_copied")
        logit_turned = sem("la_logit_turned")
        choice_step = sem("la_choice_step")
        downed = sem("la_downed")
        masked = sem("la_masked")
        reduced = sem("la_reduced")
        less_ready = sem("la_less_ready")
        exp_ready = sem("la_exp_ready")
        totalled = sem("la_totalled")
        shared = sem("la_shared")
        scaled = sem("la_scaled")
        finished = sem("la_finished")
        stored = [sem(f"la_stored{i}") for i in range(2)]
        hb = halves(P["h"][:, :], B)
        cols = lambda t, c: t[:, c * GT:(c + 1) * GT]
        v3 = lambda t: t[:, :].rearrange("p (b e) -> p b e", e=NE)
        STEPS = 7
        RUN = (-1, NG, 3, NG - 2)

        with nc.Block() as block:
            @block.sync
            def _(sp):
                def body(g, q, edge):
                    if within(edge, 1):
                        sp.wait_ge(finished, g)
                        sp.dma_start(A["out"][bass.ds((g - 1) * GB, GB)].rearrange("b t d -> t b d"),
                                     hb[:, bass.ds((g - 1) * GB, GB), :]).then_inc(stored[1 - q], 16)
                run_bodies(sp, body, *RUN)
                for s in stored:
                    sp.wait_ge(s, 16 * (NG // 2))

            @block.gpsimd
            def _(pool):
                def body(g, q, edge):
                    if within(edge, -1):
                        pool.wait_ge(choice_step, (g + 2) * STEPS)
                        if at_least(edge, -1, 2):
                            pool.wait_ge(exp_ready, g)
                        nc.gpsimd.tensor_tensor(v3(less[1 - q]), v3(small), over(largest[:, :], NE),
                                                ALU.subtract).then_inc(less_ready, 1)
                    if within(edge, 1):
                        pool.wait_ge(shared, g)
                        pool.wait_ge(reduced, g * GB)
                        yv = halves(y[1 - q][:, :], GB)
                        nc.gpsimd.tensor_tensor(yv, yv, over(share[1 - q][:, :], D), ALU.mult).then_inc(scaled, 1)
                        pool.wait_ge(scaled, g)
                        at = P["h"][:, bass.ds((g - 1) * GB * D, GB * D)]
                        nc.gpsimd.tensor_tensor(at, at, y[1 - q][:, :], ALU.add).then_inc(finished, 1)
                run_bodies(pool, body, *RUN)

            @block.tensor
            def _(pe):
                def down(g, q, b, edge):
                    n = g * GB + b
                    if b == 0:
                        pe.wait_ge(low, (g + 1) * HC)
                    if at_least(edge, 0, 1):
                        pe.wait_ge(masked, n - 3)
                    out = ps_y[b][0:T, :]
                    tb = lambda c: slice(c * GT + b * T, c * GT + (b + 1) * T)
                    wc = lambda c: slice(c * 512, (c + 1) * 512)
                    nc.tensor.matmul(out, P["ones"][:, :], P["down2_bias"][:, :], start=True, stop=False)
                    for c in range(HC):
                        nc.tensor.matmul(out, hh[q][:, tb(c)], P["down2_high"][:, wc(c)], start=False, stop=False)
                        nc.tensor.matmul(out, hh[q][:, tb(c)], P["down2_low"][:, wc(c)], start=False, stop=False)
                        last = nc.tensor.matmul(out, hl[q][:, tb(c)], P["down2_high"][:, wc(c)], start=False,
                                                stop=(c == HC - 1))
                    last.then_inc(downed, 1)

                def body(g, q, edge):
                    ahead = within(edge, -1)
                    if ahead:
                        for c in range(HC):
                            if at_least(edge, -1, 1):
                                pe.wait_ge(activated, g * HC + (c + 1))
                            x = P["xs"][:, bass.ds((g + 1) * GT, GT)]
                            nc.tensor.matmul(ps_up[c][:, 0:GT], P["up2_high"][:, c * 128:(c + 1) * 128], x,
                                             start=True, stop=False)
                            nc.tensor.matmul(ps_up[c][:, 0:GT], P["up2_low"][:, c * 128:(c + 1) * 128], x,
                                             start=False, stop=True).then_inc(upped, 1)
                    if within(edge, 0):
                        down(g, q, 0, edge)
                        down(g, q, 1, edge)
                    if ahead:
                        pe.wait_ge(low, (g + 2) * HC)
                        if at_least(edge, -1, 1):
                            pe.wait_ge(logit_copied, g + 1)
                        for c in range(HC):
                            for h in (hh, hl):
                                last = nc.tensor.matmul(ps_logit[:, 0:GT], P["gate2"][:, c * 128:(c + 1) * 128],
                                                        cols(h[1 - q], c), start=(c == 0 and h is hh),
                                                        stop=(c == HC - 1 and h is hl))
                        last.then_inc(scored, 1)
                    if within(edge, 0):
                        down(g, q, 2, edge)
                    if ahead:
                        pe.wait_ge(logit_copied, g + 2)
                        if at_least(edge, -1, 1):
                            pe.wait_ge(choice_step, (g + 1) * STEPS)
                        for b in range(GB):
                            last = nc.tensor.transpose(ps_turn[0:T, b * 128:(b + 1) * 128],
                                                       lt[:, b * T:(b + 1) * T], P["ident"][:, :])
                        last.then_inc(logit_turned, 1)
                    if within(edge, 0):
                        down(g, q, 3, edge)
                run_bodies(pe, body, *RUN)

            @block.scalar
            def _(act):
                def hidden_units(g, q, edge):
                    for c in range(HC):
                        if at_least(edge, -1, 1):
                            act.wait_ge(low, g * HC + (c + 1))
                        act.wait_ge(upped, (g + 1) * HC + (c + 1))
                        nc.scalar.activation(cols(hidden, c), ps_up[c][:, 0:GT], ACT.Gelu,
                                             bias=P["up2_bias"][:, c:c + 1]).then_inc(activated, 1)
                    if at_least(edge, -1, 2):
                        act.wait_ge(downed, g * GB)
                    for c in range(HC):
                        act.wait_ge(activated, (g + 1) * HC + (c + 1))
                        nc.scalar.activation(cols(hh[1 - q], c), cols(hidden, c), ACT.Copy).then_inc(high, 1)
                    act.wait_ge(scored, g + 2)
                    if at_least(edge, -1, 1):
                        act.wait_ge(logit_turned, g + 1)
                    nc.scalar.activation(lt[:, :], ps_logit[:, 0:GT], ACT.Copy).then_inc(logit_copied, 1)

                def body(g, q, edge):
                    if within(edge, 1):
                        act.wait_ge(less_ready, g)
                        if at_least(edge, 1, 1):
                            act.wait_ge(totalled, g - 1)
                        nc.scalar.activation(exps[:, :], less[1 - q][:, :], ACT.Exp).then_inc(exp_ready, 1)
                    if within(edge, -1):
                        hidden_units(g, q, edge)
                run_bodies(act, body, *RUN)

            @block.vector
            def _(dve):
                def rest(g, q, c):
                    dve.wait_ge(high, g * HC + (c + 1))
                    nc.vector.tensor_tensor(cols(hl[q], c), cols(hidden, c), cols(hh[q], c).bitcast(F32),
                                            ALU.subtract).then_inc(low, 1)

                def choose(g, q, edge):
                    dve.wait_ge(logit_turned, g + 1)
                    if at_least(edge, 0, 1):
                        dve.wait_ge(less_ready, g)
                    k = [0]

                    def step(ins):
                        k[0] += 1
                        ins.then_inc(choice_step, 1)
                        dve.wait_ge(choice_step, g * STEPS + k[0])

                    step(nc.vector.tensor_reduce(
                        v3(small), ps_turn[0:T, :].rearrange("p (b n) -> p b n", b=GB)[:, :, 0:2 * NE]
                        .rearrange("p b (two e) -> p b e two", two=2),
                        axis=AX_X, op=ALU.add))
                    step(nc.vector.tensor_tensor(v3(small), v3(small),
                                                 P["gate2_bias"][:, :].unsqueeze(1).to_broadcast([T, GB, NE]), ALU.add))
                    first_argmax(nc, step, v3(small), P["rank"][:, :], largest[:, :], top[:, :], v3(ties), v3(chosen[q]), (T, GB))
                    assert k[0] == STEPS

                def pick(g, q, b, edge):
                    n = g * GB + b
                    if at_least(edge, 0, 1):
                        dve.wait_ge(reduced, n - (GB - 1))
                    dve.wait_ge(downed, n + 1)
                    nc.vector.tensor_tensor(picked[b][:, :].rearrange("p (e c) -> p e c", e=NE),
                                            ps_y[b][0:T, :].rearrange("p (e c) -> p e c", e=NE),
                                            over(chosen[q][:, b * NE:(b + 1) * NE], D), ALU.mult).then_inc(masked, 1)
                    if edge is None or edge * GB + b >= 1:
                        dve.wait_ge(masked, n)
                        reduce(g if b else g - 1, q if b else 1 - q, (b - 1) % GB, edge)

                def reduce(g, q, b, edge):
                    if b == 0 and at_least(edge, 0, 2):
                        dve.wait_ge(finished, g - 1)
                    nc.vector.tensor_reduce(y[q][:, b * D:(b + 1) * D],
                                            picked[b][:, :].rearrange("p (e c) -> p c e", e=NE),
                                            axis=AX_X, op=ALU.add).then_inc(reduced, 1)

                def probability(g, q):
                    dve.wait_ge(exp_ready, g + 1)
                    nc.vector.tensor_reduce(total[:, :], v3(exps), axis=AX_X, op=ALU.add).then_inc(totalled, 1)
                    dve.wait_ge(totalled, g + 1)
                    nc.vector.reciprocal(share[q][:, :], total[:, :]).then_inc(shared, 1)

                def body(g, q, edge):
                    ahead, main = within(edge, -1), within(edge, 0)
                    if ahead:
                        rest(g + 1, 1 - q, 0)
                        rest(g + 1, 1 - q, 1)
                    if main:
                        pick(g, q, 0, edge)
                    if within(edge, 1):
                        probability(g - 1, 1 - q)
                    if main:
                        pick(g, q, 1, edge)
                        pick(g, q, 2, edge)
                    if ahead:
                        choose(g + 1, 1 - q, None if edge is None else edge + 1)
                    if main:
                        pick(g, q, 3, edge)
                    if edge == NG - 1:
                        dve.wait_ge(masked, B)
                        reduce(g, q, GB - 1, edge)
                run_bodies(dve, body, *RUN)


def program(nc, A):
    tok_dram = nc.dram_tensor("tok_dram", (B, TI, D), F32, kind="Internal").ap()
    gates_dram = nc.dram_tensor("gates_dram", (8 * 2 * NE, B // 8 * T), F32, kind="Internal").ap()
    cpad_dram = nc.dram_tensor("cpad_dram", (D, 2 * T), F32, kind="Internal").ap()
    with ExitStack() as ctx:
        def sb(name, shape, dt=F32):
            return ctx.enter_context(nc.sbuf_tensor(name, shape, dt))

        def sem(name):
            return ctx.enter_context(nc.semaphore(name))

        P = dict(
            h=sb("h", [T, B * D]),
            up_high=sb("up_high", [128, NE * D], F32R), up_low=sb("up_low", [128, NE * D], F32R),
            router=sb("router", [128, 2 * NE], F32R),
            down=sb("down", [128, CH * D]), up_bias=sb("up_bias", [128, CH]), down_bias=sb("down_bias", [2 * NE, D]),
            sel=sb("sel", [2 * NE, CH * 128], F32R),
            score_high=sb("score_high", [128, HEADS * D], F32R), score_low=sb("score_low", [128, HEADS * D], F32R),
            value=sb("value", [128, CH * D]),
            up2_high=sb("up2_high", [128, HID], F32R), up2_low=sb("up2_low", [128, HID], F32R),
            up2_bias=sb("up2_bias", [128, HC]),
            gate2=sb("gate2", [128, HC * 128], F32R), gate2_bias=sb("gate2_bias", [T, NE]),
            down2_high=sb("down2_high", [128, HC * NE * D], F32R), down2_low=sb("down2_low", [128, HC * NE * D], F32R),
            down2_bias=sb("down2_bias", [33, NE * D], F32R), ones=sb("ones", [33, T], F32R),
            ident=sb("ident", [128, 128]), rank=sb("rank", [T, NE]),
            norm_consts=[sb(f"norm_consts{i}", [T, LB]) for i in range(2)],
            tokens_stored=[sem(f"tokens_stored{i}") for i in range(4)],
            tokens_arrived=[sem(f"tokens_arrived{i}") for i in range(4)], text_arrived=sem("text_arrived"),
            tok_dram=tok_dram, cpad_dram=cpad_dram, gates=gates_dram)

        def phase(fn):
            with ExitStack() as banks:
                fn(nc, sb, lambda name, shape: banks.enter_context(nc.psum_tensor(name, shape, F32)), sem, A, P)

        with ExitStack() as early:
            for name, shape in (("wq_raw", [128, D * HEADS]), ("wk_raw", [128, D * HEADS]),
                                ("wv_raw", [128, D * HEADS]), ("wo_raw", [D, HEADS * D])):
                P[name] = early.enter_context(nc.sbuf_tensor(name, shape, F32))
            P["token_tiles"] = [early.enter_context(nc.sbuf_tensor(f"token_tile{i}", [128, G8 * D], F32))
                                for i in range(4)]
            phase(front)
            phase(convolution)
        P["xs"] = sb("xs", [128, B * T], F32R)
        phase(route)
        P["xn"] = sb("xn_all", [T, B * D])
        phase(experts)
        phase(attention)
        phase(last_layer)



def _resize(n):
    scale = n / G8
    centre = (np.arange(G8) + 0.5) * scale - 0.5
    w = np.maximum(0.0, 1.0 - np.abs(centre[:, None] - np.arange(n)[None, :]) / max(scale, 1.0))
    return w / w.sum(1, keepdims=True)


def _constants():
    def haar(n, sign):
        m = np.zeros((n // 2, n))
        m[np.arange(n // 2), np.arange(0, n, 2)] = 0.7071067811865476
        m[np.arange(n // 2), np.arange(1, n, 2)] = sign * 0.7071067811865476
        return m

    half, quarter = IMG // 2, IMG // 4
    lo1, hi1 = haar(IMG, 1), haar(IMG, -1)
    filt = [_resize(quarter) @ haar(half, 1) @ lo1, _resize(quarter) @ haar(half, -1) @ lo1,
            _resize(half) @ lo1, _resize(half) @ hi1]
    rows = np.concatenate([f.T for f in filt], 1)
    maps = [(0, 0), (1, 0), (0, 1), (1, 1), (3, 2), (2, 3), (3, 3)]
    cols = np.zeros((IMG, 4, NMAP, G8))
    for m, (r, c) in enumerate(maps):
        cols[:, r, m, :] = filt[c].T
    sel = np.zeros((2, NE, CH, 2, D))
    for e in range(NE):
        sel[:, e, e // 2, e % 2, :] = 1.0
    f = np.float32
    return {"c_rows": rows.astype(f), "c_cols": cols.reshape(IMG, -1).astype(f), "c_ident": np.eye(128, dtype=f),
            "c_rank": np.tile(NE - np.arange(NE, dtype=f), (T, 1)), "c_sel": sel.reshape(2 * NE, CH * 128).astype(f)}


_INS = ['x', 'txt', 'L0_tok_W', 'L0_tok_b', 'L0_attn_c', 'L0_ffn_router_w', 'L0_ffn_w1', 'L0_ffn_b1', 'L0_ffn_w2',
        'L0_ffn_b2', 'L1_attn_Wq', 'L1_attn_Wk', 'L1_attn_Wv', 'L1_attn_Wo', 'L1_ffn_W1', 'L1_ffn_b1', 'L1_ffn_Wg',
        'L1_ffn_bg', 'L1_ffn_Wd', 'L1_ffn_bd']


def kernel(**inputs):
    import concourse.bacc as bacc
    from concourse.bass_utils import run_bass_kernel_spmd

    nc = bacc.Bacc("TRN2", target_bir_lowering=False, num_devices=1)
    arrays, A = {}, {}
    for name, a in [(n, inputs[n]) for n in _INS] + list(_constants().items()):
        a = np.ascontiguousarray(a)
        arrays[f"in_{name}"] = a
        A[name] = nc.dram_tensor(f"in_{name}", a.shape, mybir.dt.from_np(a.dtype), kind="ExternalInput").ap()
    A["out"] = nc.dram_tensor("out_0", (B, T, D), F32, kind="ExternalOutput").ap()
    program(nc, A)
    r = run_bass_kernel_spmd(nc, [arrays], core_ids=[0])
    return r.results[0]["out_0"]
```
